# Optimizing a Trainium2 kernel written in Bass

```python
import numpy as np
import jax
import jax.numpy as jnp

def _softmax(x, axis=-1):
    return jax.nn.softmax(x, axis=axis)

def _gelu(x):
    return jax.nn.gelu(x, approximate=True)

def _silu(x):
    return jax.nn.silu(x)

def _sigmoid(x):
    return jax.nn.sigmoid(x)

def _layernorm(x, axis=-1, eps=1e-05):
    m = jnp.mean(x, axis=axis, keepdims=True)
    v = jnp.var(x, axis=axis, keepdims=True)
    return (x - m) / jnp.sqrt(v + eps)

def _scatter_add(tgt, idx, src, axis=0):
    return tgt.at[idx].add(src)

def _segment_sum(src, seg, n):
    return jax.ops.segment_sum(src, seg, n)
kernel_name = 'mk_macaron_d1_jaxref_r4_1bcb00'

def setup_inputs(seed: int=0):
    np.random.seed(seed)
    _w = jnp.asarray

    def _L0_attn_setup():
        import jax, jax.numpy as jnp
        import numpy as np
        HEADS, D_MODEL, D_V = (16, 256, 64)
        D_K = D_MODEL // HEADS
        key = jax.random.key(seed)
        k1, k2, k3, k4, k5 = jax.random.split(key, 5)
        B, T = (2, 512)
        s = 1.0 / np.sqrt(D_MODEL)
        return {'x': jax.random.normal(k1, (B, T, D_MODEL), dtype=jnp.float32), 'Wq': jax.random.normal(k2, (D_MODEL, HEADS * D_K), dtype=jnp.float32) * s, 'Wk': jax.random.normal(k3, (D_MODEL, HEADS * D_K), dtype=jnp.float32) * s, 'Wv': jax.random.normal(k4, (D_MODEL, HEADS * D_V), dtype=jnp.float32) * s, 'Wo': jax.random.normal(k5, (HEADS * D_V, D_MODEL), dtype=jnp.float32) * (1.0 / np.sqrt(HEADS * D_V))}
    _L0_attn_in = _L0_attn_setup()

    def _L0_ffn_setup():
        import jax, jax.numpy as jnp
        import numpy as np
        E = 8
        K = 2
        C = 256
        F = 512
        EPS = 1e-05
        key = jax.random.key(seed)
        ks = jax.random.split(key, 6)
        x = jax.random.normal(ks[0], (2, 256, C), dtype=jnp.float32)
        ln_gamma = 1.0 + 0.02 * jax.random.normal(ks[1], (C,), dtype=jnp.float32)
        ln_beta = 0.02 * jax.random.normal(ks[2], (C,), dtype=jnp.float32)
        gate_w = jax.random.normal(ks[3], (E, C), dtype=jnp.float32) / np.sqrt(C)
        w1 = jax.random.normal(ks[4], (E, F, C), dtype=jnp.float32) / np.sqrt(C)
        w2 = jax.random.normal(ks[5], (E, C, F), dtype=jnp.float32) / np.sqrt(F)
        return {'x': x, 'ln_gamma': ln_gamma, 'ln_beta': ln_beta, 'gate_w': gate_w, 'w1': w1, 'w2': w2}
    _L0_ffn_in = _L0_ffn_setup()
    _d = {'L0_attn_x': _L0_attn_in['x'], 'L0_attn_Wq': _L0_attn_in['Wq'], 'L0_attn_Wk': _L0_attn_in['Wk'], 'L0_attn_Wv': _L0_attn_in['Wv'], 'L0_attn_Wo': _L0_attn_in['Wo'], 'L0_ffn_ln_gamma': _L0_ffn_in['ln_gamma'], 'L0_ffn_ln_beta': _L0_ffn_in['ln_beta'], 'L0_ffn_gate_w': _L0_ffn_in['gate_w'], 'L0_ffn_w1': _L0_ffn_in['w1'], 'L0_ffn_w2': _L0_ffn_in['w2']}
    _x0 = _d['L0_attn_x']
    _d['L0_attn_x'] = jax.random.normal(jax.random.fold_in(jax.random.key(seed), 1), (8, 512, 256), dtype=_x0.dtype)
    del _x0
    return _d

def reference(L0_attn_x, L0_attn_Wq, L0_attn_Wk, L0_attn_Wv, L0_attn_Wo, L0_ffn_ln_gamma, L0_ffn_ln_beta, L0_ffn_gate_w, L0_ffn_w1, L0_ffn_w2):

    def _L0_attn_ref(x, Wq, Wk, Wv, Wo):
        import jax, jax.numpy as jnp
        import numpy as np
        HEADS, D_MODEL, D_V = (16, 256, 64)
        D_K = D_MODEL // HEADS
        B, T, _ = x.shape
        scale = jnp.asarray(np.sqrt(D_K), x.dtype)
        q = (x @ Wq).reshape(B, T, HEADS, D_K).transpose(0, 2, 1, 3)
        k = (x @ Wk).reshape(B, T, HEADS, D_K).transpose(0, 2, 1, 3)
        v = (x @ Wv).reshape(B, T, HEADS, D_V).transpose(0, 2, 1, 3)
        scores = jnp.einsum('bhqd,bhkd->bhqk', q, k) / scale
        causal = jnp.triu(jnp.ones((T, T), dtype=bool), k=1)
        scores = jnp.where(causal, jnp.asarray(-jnp.inf, scores.dtype), scores)
        attn = jax.nn.softmax(scores, axis=-1)
        ctx = jnp.einsum('bhqk,bhkd->bhqd', attn, v)
        out = ctx.transpose(0, 2, 1, 3).reshape(B, T, HEADS * D_V)
        return out @ Wo

    def _L0_ffn_ref(x, ln_gamma, ln_beta, gate_w, w1, w2):
        import jax, jax.numpy as jnp
        import numpy as np
        E = 8
        K = 2
        C = 256
        F = 512
        EPS = 1e-05
        B, T, Cc = x.shape
        xf = x.reshape(-1, Cc)
        mu = jnp.mean(xf, axis=-1, keepdims=True)
        var = jnp.var(xf, axis=-1, keepdims=True)
        rn = (xf - mu) * jax.lax.rsqrt(var + EPS) * ln_gamma + ln_beta
        logits = rn @ gate_w.T
        probs = jax.nn.softmax(logits, axis=-1)
        rw, sel = jax.lax.top_k(probs, K)
        comb = jnp.sum(jax.nn.one_hot(sel, E, dtype=xf.dtype) * rw[..., None], axis=1)
        h = jax.nn.gelu(jnp.einsum('nc,efc->enf', xf, w1), approximate=False)
        y = jnp.einsum('enf,ecf->enc', h, w2)
        out = jnp.einsum('enc,ne->nc', y, comb)
        return out.reshape(B, T, Cc)
    x = L0_attn_x
    x = x + 0.5 * _L0_ffn_ref(_layernorm(x, axis=-1), L0_ffn_ln_gamma, L0_ffn_ln_beta, L0_ffn_gate_w, L0_ffn_w1, L0_ffn_w2)
    x = x + _L0_attn_ref(_layernorm(x, axis=-1), L0_attn_Wq, L0_attn_Wk, L0_attn_Wv, L0_attn_Wo)
    x = x + 0.5 * _L0_ffn_ref(_layernorm(x, axis=-1), L0_ffn_ln_gamma, L0_ffn_ln_beta, L0_ffn_gate_w, L0_ffn_w1, L0_ffn_w2)
    return x

_drawn_inputs = setup_inputs


def setup_inputs(seed=0):
    import zlib

    import numpy as np

    out = dict(_drawn_inputs(seed))
    spreads = {}
    factors = {'L0_ffn_ln_gamma': 10.276, 'L0_ffn_ln_beta': 9.339}
    for name, (base, spread) in spreads.items():
        noise = np.random.default_rng([zlib.crc32(name.encode()), seed]).standard_normal(out[name].shape)
        drawn = base * np.exp(spread * noise) if base else spread * noise
        out[name] = jnp.asarray(drawn.astype(out[name].dtype))
    for name, factor in factors.items():
        out[name] = (out[name] * factor).astype(out[name].dtype)
    return out
```

```python
from contextlib import ExitStack

import concourse.bass as bass
from concourse import mybir

ALU = mybir.AluOpType
ACT = mybir.ActivationFunctionType
AX = mybir.AxisListType
F32 = mybir.dt.float32
F32R = mybir.dt.float32r
BF16 = mybir.dt.bfloat16
I32 = mybir.dt.int32

P = 128
B, T, C = 8, 512, 256
N = B * T
NT = N // P
TB = T // P
KC = C // P
E, TOPK, F = 8, 2, 512
KF = F // P
NS = N * TOPK // P + E
EPS = 1e-5
WE = KC * F
assert WE == KF * C
HEADS, DK, DV = 16, 16, 64
NEG = -3.0e38


class Steps:

    def __init__(self, eng, sem):
        self.eng, self.sem, self.base, self.k = eng, sem, 0, 0

    def did(self, ins):
        ins.then_inc(self.sem, 1)
        self.k += 1

    def settle(self):
        self.eng.wait_ge(self.sem, self.base + self.k)

    def loop(self, start, end, per, body):
        first = self.base + self.k
        with self.eng.Fori(start, end) as i:
            self.base, self.k = i * per + (first - start * per), 0
            body(i)
            assert self.k == per, (self.k, per)
        self.base, self.k = first + (end - start) * per, 0


def split_pass(nc, out, hi, lo, rhi, rlo, start, stop):
    nc.tensor.matmul(out, lo, rhi, start=start, stop=False)
    nc.tensor.matmul(out, hi, rlo, start=False, stop=False)
    return nc.tensor.matmul(out, hi, rhi, start=False, stop=stop)


def at_least(n):
    return max(n, 0) if isinstance(n, int) else n


class Core:

    def __init__(self, nc, ctx, ins):
        self.nc, self.ins = nc, ins

        def sb(name, shape, dt):
            return ctx.enter_context(nc.sbuf_tensor(name, shape, dt))

        def sem(name):
            return ctx.enter_context(nc.semaphore(name))

        self.sem = sem
        psum = ctx.enter_context(nc.psum_tensor("psum", [P, 8, 512], F32))
        self.bank = [psum[:, i, :] for i in range(8)]
        self.sets = [psum[:, 3 * i:3 * i + 3, :].rearrange("p a b -> p (a b)") for i in range(2)]
        self.x = sb("x_rows", [P, NT, C], F32)
        self.ident = sb("ident", [P, P], F32)
        self.before = sb("before", [P, P], BF16)
        self.ones = sb("ones", [P, P], BF16)
        self.zeros = sb("zeros", [P, 2 * NS], BF16)
        self.slot_iota = sb("slot_iota", [P, P], BF16)
        self.e_iota = sb("e_iota", [P, E], F32)
        self.t_col = sb("t_col", [P, NT], F32)
        self.p_col = sb("p_col", [P, 1], F32)
        self.fresh = sb("fresh", [P, E, NT], F32)
        self.gw = sb("gw", [P, KC, E], F32)
        self.gamma = sb("gamma", [P, KC], F32)
        self.beta = sb("beta", [P, KC], F32)
        self.beta_rep = sb("beta_rep", [P, KC, P], F32)
        self.minus_half = sb("minus_half", [P, NT], F32)
        self.x_rows = sem("x_loaded")
        self.small = sem("small_loaded")
        self.const = sem("const_ready")
        self.beta_ready = sem("beta_ready")

    CONSTS = 12

    def sync(self, sp):
        x = self.ins["x"].rearrange("(t p) c -> p t c", p=P)
        for g in range(2):
            h = NT // 2
            sp.dma_start(self.x[:, g * h:(g + 1) * h, :], x[:, g * h:(g + 1) * h, :]).then_inc(self.x_rows, 16)
        sp.dma_start(self.gw[:], self.ins["gate"]).then_inc(self.small, 16)
        sp.dma_start(self.gamma[:], self.ins["gamma"]).then_inc(self.small, 16)
        sp.dma_start(self.beta[:], self.ins["beta"]).then_inc(self.small, 16)

    def pool(self, pool):
        c = Steps(pool, self.const)
        c.did(pool.memset(self.minus_half[:], -0.5))
        c.did(pool.memset(self.ident[:], 0.0))
        c.did(pool.memset(self.before[:], 1.0))
        c.did(pool.memset(self.ones[:], 1.0))
        c.did(pool.memset(self.zeros[:], 0.0))
        c.did(pool.memset(self.fresh[:], 1.0))
        c.did(pool.iota(self.slot_iota[:], pattern=[[1, P]], base=0, channel_multiplier=0,
                        allow_small_or_imprecise_dtypes=True))
        c.did(pool.iota(self.e_iota[:], pattern=[[1, E]], base=-E, channel_multiplier=0,
                        allow_small_or_imprecise_dtypes=True))
        c.did(pool.iota(self.t_col[:], pattern=[[1, NT]], base=0, channel_multiplier=0,
                        allow_small_or_imprecise_dtypes=True))
        c.did(pool.iota(self.p_col[:], pattern=[[0, 1]], base=0, channel_multiplier=1,
                        allow_small_or_imprecise_dtypes=True))
        c.settle()
        c.did(pool.affine_select(out=self.ident[:], in_=self.ident[:], compare_op=ALU.not_equal, fill=1.0,
                                 base=0, pattern=[[-1, P]], channel_multiplier=1))
        c.did(pool.affine_select(out=self.before[:], in_=self.before[:], compare_op=ALU.is_gt, fill=0.0,
                                 base=0, pattern=[[1, P]], channel_multiplier=-1))
        c.settle()
        assert c.k == self.CONSTS

    def vector(self, dve):
        dve.wait_ge(self.const, self.CONSTS)
        dve.wait_ge(self.small, 48)
        dve.memset(self.fresh[:, :, 0:1], 0.0).then_inc(self.beta_ready, 1)
        for k in range(KC):
            dve.tensor_scalar(self.beta_rep[:, k, :], self.ident[:], 0.0, self.beta[:, k:k + 1],
                              ALU.mult, ALU.add).then_inc(self.beta_ready, 1)
        dve.wait_ge(self.beta_ready, 1 + KC)


class MoeMemory:

    def __init__(self, nc, ctx):
        def sb(name, shape, dt):
            return ctx.enter_context(nc.sbuf_tensor(name, shape, dt))

        with nc.sbuf_tensor("y_gathered", [P, 2, 4, TOPK, C], F32) as yg:
            self.yg = [yg[:, i, :, :, :] for i in range(2)]
        self.w1 = [sb(f"w1_{x}", [P, E * WE], F32R) for x in ("hi", "lo")]
        self.w2 = [sb(f"w2_{x}", [P, E * WE], F32R) for x in ("hi", "lo")]
        self.staged = [sb(f"staged{i}", [P, 1024], F32) for i in range(2)]
        self.pos = sb("pos", [P, NT * TOPK], I32)
        self.weight = sb("weight", [P, TOPK, NT], F32)
        self.woff = sb("woff", [P, NS], I32)
        self.ids = sb("ids", [P, NS], I32)
        self.idc = [sb(f"idc{i}", [P, 4 * TOPK], I32) for i in range(2)]
        te = [P, NT, E]
        with ExitStack() as ctx:
            self.stats = sb("stats", [P, 4, 6], F32)
            self.mv = sb("mv", [P, 2, NT], F32)
            self.mv4 = sb("mv4", [P, 2, 4], F32)
            self.var = sb("var_eps", [P, NT], F32)
            self.rstd = sb("rstd", [P, NT], F32)
            self.rr = sb("rr", [P, NT], F32)
            self.var2 = sb("var2_eps", [P, NT], F32)
            self.rstd2 = sb("rstd2", [P, NT], F32)
            self.xf = [sb(f"xf{i}", [P, 4, C], F32) for i in range(2)]
            self.xgt = [sb(f"xgt{i}", [P, KC, P], F32) for i in range(2)]
            self.logits = sb("logits", te, F32)
            self.ex = sb("ex", te, F32)
            self.eq = sb("eq", te, F32)
            self.oh = [sb(f"oh{i}", te, F32) for i in range(2)]
            self.row = sb("row", [P, NT], F32)
            self.best = [sb(f"best{i}", [P, NT], F32) for i in range(2)]
            self.rinv = sb("rinv", [P, NT], F32)
            self.chosen = sb("chosen", [P, E, NT], BF16)
            self.incl = sb("incl", [P, E, NT], F32)
            self.place = sb("place", [P, E, NT], F32)
            self.cnt = sb("cnt", [P, E], I32)
            self.tiles_i = sb("tiles_i", [P, E], I32)
            self.tiles = sb("tiles", [P, E], F32)
            self.endt = sb("endt", [P, E], F32)
            self.base = sb("base", [P, E], F32)
            self.posf = sb("posf", [P, NT, TOPK], F32)
            self.slot_i = sb("slot_i", [P, NT * TOPK], I32)
            self.slot = sb("slot", [P, NT * TOPK], F32)
            self.lane = sb("lane", [P, NT * TOPK], F32)
            self.past = sb("past", [P, NS, E], BF16)
            self.wsel = sb("wsel", [P, NS], F32)
            self.hot = [sb(f"hot{i}", [P, TOPK, P], BF16) for i in range(2)]
            self.vals = [sb(f"vals{i}", [P, TOPK, 2, NS], BF16) for i in range(2)]
            self.idf = sb("idf", [P, NS], F32)
        with ExitStack() as ctx:
            self.idb = [sb(f"idb{i}", [P, 1], I32) for i in range(2)]
            self.xg = [sb(f"xg{i}", [P, C], F32) for i in range(2)]
            self.xt = [[sb(f"xt{i}_{x}", [P, C], F32R) for x in ("hi", "lo")] for i in range(2)]
            self.h = [sb(f"h{i}", [P, F], F32) for i in range(2)]
            self.ht = [[sb(f"ht{i}_{x}", [P, F], F32R) for x in ("hi", "lo")] for i in range(2)]
            self.y = [sb(f"y{i}", [P, C], F32) for i in range(2)]


class Moe:

    CH = 1024
    NCH = E * WE // CH

    def __init__(self, core, mem, tag):
        nc, self.c, self.m = core.nc, core, mem
        self.nc = nc
        self.xf_d = nc.dram_tensor(f"{tag}_xf", [N, C], F32, kind="Internal")
        self.y_d = nc.dram_tensor(f"{tag}_y", [NS * P, C], F32, kind="Internal")

        def sem(name):
            return core.sem(f"{tag}_{name}")

        def two(name):
            return [sem(f"{name}{i}") for i in range(2)]

        self.staged_in = two("staged_in")
        self.hi_done = sem("hi_done")
        self.lo_done = sem("lo_done")
        self.dve_step = sem("dve_step")
        self.var_ready = sem("var_ready")
        self.rstd_ready = sem("rstd_ready")
        self.xf_ready = sem("xf_ready")
        self.xf_stored = two("xf_stored")
        self.xf_turned = two("xf_turned")
        self.xf_in_psum = sem("xf_in_psum")
        self.xgt_ready = two("xgt_ready")
        self.xgt_used = two("xgt_used")
        self.logits_done = sem("logits_done")
        self.shifted = sem("shifted")
        self.ex_ready = sem("ex_ready")
        self.chosen_ready = sem("chosen_ready")
        self.ranked = sem("ranked")
        self.hot_ready = sem("hot_ready")
        self.hot_used = two("hot_used")
        self.ids_done = sem("ids_done")
        self.ids_ready = sem("ids_ready")
        self.idb_ready = sem("idb_ready")
        self.waited = sem("waited")
        self.dve_waited = sem("dve_waited")
        self.gathered = two("gathered")
        self.xg_used = two("xg_used")
        self.xt_hi = sem("xt_hi")
        self.xt_lo = sem("xt_lo")
        self.h_done = sem("h_done")
        self.gelu_done = sem("gelu_done")
        self.h_turned = sem("h_turned")
        self.ht_hi = sem("ht_hi")
        self.ht_lo = sem("ht_lo")
        self.y_done = sem("y_done")
        self.y_ready = sem("y_ready")
        self.y_stored = two("y_stored")
        self.idc_ready = sem("idc_ready")
        self.y_back = two("y_back")
        self.yg_used = two("yg_used")
        self.x_done = sem("x_done")

    def sync(self, sp):
        self.load_weights(sp, range(2))
        rows = self.xf_d[:].rearrange("(t p) c -> p t c", p=P)
        with sp.Fori(0, NT // 8) as i:
            for p in range(2):
                sp.wait_ge(self.c.x_rows, 32)
                sp.wait_ge(self.xf_ready, 8 * i + 4 * (p + 1))
                sp.dma_start(rows[:, bass.ds(8 * i + 4 * p, 4), :], self.m.xf[p][:]).then_inc(self.xf_stored[p], 16)
        self.load_weights(sp, range(2, 2 * self.NCH))
        self.sync_y(sp)

    def load_weights(self, sp, chunks):
        m = self.m
        for n in chunks:
            src, c = (self.c.ins["w1"], n) if n < self.NCH else (self.c.ins["w2"], n - self.NCH)
            if n >= 2:
                sp.wait_ge(self.lo_done, n - 1)
            sp.dma_start(m.staged[n % 2][:], src[:, c * self.CH:(c + 1) * self.CH])\
              .then_inc(self.staged_in[n % 2], 16)

    def sync_y(self, sp):
        m = self.m
        with sp.Fori(0, NS // 2) as i:
            for p in range(2):
                sp.wait_ge(self.c.x_rows, 32)
                sp.wait_ge(self.y_ready, 2 * i + (p + 1))
                sp.dma_start(self.y_d[bass.ds(i * (2 * P) + p * P, P), :], m.y[p][:])\
                  .then_inc(self.y_stored[p], 16)

    def act_split(self, act):
        m = self.m
        for n in range(2 * self.NCH):
            w, c = (m.w1, n) if n < self.NCH else (m.w2, n - self.NCH)
            act.wait_ge(self.staged_in[n % 2], 16 * (n // 2 + 1))
            act.activation(w[0][:, c * self.CH:(c + 1) * self.CH], m.staged[n % 2][:], ACT.Copy)\
               .then_inc(self.hi_done, 1)

    def act_xgt(self, act):
        m, bank = self.m, self.c.bank
        with act.Fori(0, NT // 2) as i:
            for r in range(2):
                act.wait_ge(self.xf_in_psum, 2 * i + (r + 1))
                act.wait_ge(self.xgt_used[r], i)
                for k in range(KC):
                    last = act.activation(m.xgt[r][:, k, :], bank[r][:, k * P:(k + 1) * P], ACT.Copy,
                                          scale=self.c.gamma[:, k:k + 1])
                    last.then_inc(self.xgt_ready[r], 1)

    def scalar(self, act):
        act.wait_ge(self.c.small, 48)
        self.act_xgt(act)
        act.wait_ge(self.shifted, 1)
        act.activation(self.m.ex[:], self.m.logits[:], ACT.Exp).then_inc(self.ex_ready, 1)
        self.act_split(act)
        self.act_tiles(act)

    def pool(self, pool):
        m, c = self.m, self.c
        pool.wait_ge(self.var_ready, 1)
        pool.tensor_tensor(m.rstd[:], m.var[:], c.minus_half[:], ALU.pow).then_inc(self.rstd_ready, 1)
        pool.wait_ge(self.var_ready, 2)
        pool.tensor_tensor(m.rstd2[:], m.var2[:], c.minus_half[:], ALU.pow).then_inc(self.rstd_ready, 1)
        for n in range(2 * self.NCH):
            w, k = (m.w1, n) if n < self.NCH else (m.w2, n - self.NCH)
            cut = slice(k * self.CH, (k + 1) * self.CH)
            pool.wait_ge(self.hi_done, n + 1)
            pool.tensor_tensor(w[1][:, cut], m.staged[n % 2][:], w[0][:, cut].bitcast(F32), ALU.subtract)\
                .then_inc(self.lo_done, 1)
        for p in range(2):
            pool.wait_ge(self.xf_stored[p], 16 * (NT // 8))
        pool.wait_ge(self.ids_ready, 1)
        with pool.Fori(0, NS // 2) as i:
            for p in range(2):
                pool.wait_ge(self.xg_used[p], i)
                pool.tensor_copy(m.idb[p][:], m.ids[:, bass.ds(2 * i + p, 1)]).then_inc(self.idb_ready, 1)
                pool.wait_ge(self.idb_ready, 2 * i + (p + 1))
                pool.sem_inc(self.waited, 1)
                pool.indirect_dma_start(out=m.xg[p][:], out_offset=None, in_=self.xf_d[:],
                                        in_offset=bass.IndirectOffsetOnAxis(ap=m.idb[p][:, 0:1], axis=0))\
                    .then_inc(self.gathered[p], 16)
        for p in range(2):
            pool.wait_ge(self.y_stored[p], 16 * (NS // 2))
        with pool.Fori(0, NT // 8) as i:
            for p in range(2):
                g = 2 * i + p
                pool.wait_ge(self.yg_used[p], 4 * i)
                pool.tensor_copy(m.idc[p][:], m.pos[:, bass.ds(g * (4 * TOPK), 4 * TOPK)])\
                    .then_inc(self.idc_ready, 1)
                pool.wait_ge(self.idc_ready, g + 1)
                pool.sem_inc(self.waited, 1)
                for q in range(4 * TOPK):
                    pool.indirect_dma_start(out=m.yg[p][:, q // TOPK, q % TOPK, :], out_offset=None,
                                            in_=self.y_d[:],
                                            in_offset=bass.IndirectOffsetOnAxis(ap=m.idc[p][:, q:q + 1], axis=0))\
                        .then_inc(self.y_back[p], 16)

    def vector(self, dve):
        m, c, bank = self.m, self.c, self.c.bank
        s = Steps(dve, self.dve_step)
        def moments(g):
            s.settle()
            for q in range(4):
                s.did(dve.bn_stats(m.stats[:, q, :], c.x[:, bass.ds(g * 4 + q, 1), :].rearrange("p a c -> p (a c)")))
            s.settle()
            dve.sem_inc(self.dve_waited, 1)
            for q in range(4):
                s.did(dve.bn_aggr(m.mv4[:, :, q], m.stats[:, q, :]))
            s.settle()
            s.did(dve.tensor_copy(m.mv[:, :, bass.ds(g * 4, 4)], m.mv4[:]))

        s.loop(0, NT // 4, 9, moments)
        s.settle()
        dve.tensor_scalar(m.var[:], m.mv[:, 1, :], EPS, None, ALU.add).then_inc(self.var_ready, 1)
        dve.wait_ge(self.rstd_ready, 1)
        s.did(dve.tensor_tensor(m.rr[:], m.rstd[:], m.rstd[:], ALU.mult))
        s.settle()
        s.did(dve.tensor_tensor(m.rr[:], m.rr[:], m.mv[:, 1, :], ALU.mult))
        s.settle()
        dve.tensor_scalar(m.var2[:], m.rr[:], EPS, None, ALU.add).then_inc(self.var_ready, 1)
        with dve.Fori(0, NT // 8) as i:
            for p in range(2):
                dve.wait_ge(self.xf_stored[p], 16 * i)
                dve.wait_ge(self.xf_turned[p], 4 * i)
                for q in range(4):
                    t = 8 * i + (4 * p + q)
                    dve.tensor_scalar(m.xf[p][:, q, :], c.x[:, bass.ds(t, 1), :].rearrange("p a c -> p (a c)"),
                                      m.mv[:, 0, bass.ds(t, 1)], m.rstd[:, bass.ds(t, 1)],
                                      ALU.subtract, ALU.mult).then_inc(self.xf_ready, 1)
        self.route(dve, s)
        self.dve_tiles(dve)
        self.combine(dve)

    def route(self, dve, s):
        m, c, bank = self.m, self.c, self.c.bank
        te = [P, NT, E]

        def do(ins):
            s.did(ins)
            s.settle()

        def tile_wide(ap):
            return ap[:].unsqueeze(2).to_broadcast(te)

        experts = c.e_iota[:].unsqueeze(1).to_broadcast(te)
        dve.wait_ge(self.logits_done, 1)
        dve.wait_ge(self.rstd_ready, 2)
        do(dve.tensor_tensor(m.logits[:], bank[7][:, 0:NT * E].rearrange("p (t e) -> p t e", e=E),
                             tile_wide(m.rstd2), ALU.mult))
        do(dve.tensor_tensor(m.logits[:], m.logits[:], bank[6][:, 0:E].unsqueeze(1).to_broadcast(te), ALU.add))
        do(dve.tensor_reduce(m.row[:], m.logits[:], AX.X, ALU.max))
        s.did(dve.tensor_tensor(m.logits[:], m.logits[:], tile_wide(m.row), ALU.subtract))
        s.settle()
        dve.sem_inc(self.shifted, 1)
        dve.wait_ge(self.ex_ready, 1)
        do(dve.tensor_reduce(m.row[:], m.ex[:], AX.X, ALU.add))
        do(dve.reciprocal(m.rinv[:], m.row[:]))
        do(dve.tensor_scalar(m.rinv[:], m.rinv[:], 0.5, None, ALU.mult))
        for k in range(TOPK):
            do(dve.tensor_reduce(m.best[k][:], m.ex[:], AX.X, ALU.max))
            do(dve.tensor_tensor(m.weight[:, k, :], m.best[k][:], m.rinv[:], ALU.mult))
            do(dve.tensor_tensor(m.eq[:], m.ex[:], tile_wide(m.best[k]), ALU.is_equal))
            do(dve.tensor_tensor(m.eq[:], m.eq[:], experts, ALU.mult))
            do(dve.tensor_reduce(m.row[:], m.eq[:], AX.X, ALU.min))
            do(dve.tensor_tensor(m.oh[k][:], experts, tile_wide(m.row), ALU.is_equal))
            if k + 1 < TOPK:
                do(dve.scalar_tensor_tensor(out=m.ex[:], in0=m.oh[k][:], scalar=-2.0, in1=m.ex[:],
                                            op0=ALU.mult, op1=ALU.add))
        dve.tensor_tensor(m.chosen[:].rearrange("p e t -> p t e"), m.oh[0][:], m.oh[1][:], ALU.add)\
           .then_inc(self.chosen_ready, 1)
        dve.wait_ge(self.ranked, 1)
        totals = bank[4][:, 0:E * NT]
        do(dve.tensor_tensor_scan(m.incl[:].rearrange("p e t -> p (e t)"), c.fresh[:].rearrange("p e t -> p (e t)"),
                                  totals, 0.0, ALU.mult, ALU.add))
        do(dve.tensor_tensor(m.place[:].rearrange("p e t -> p (e t)"), m.incl[:].rearrange("p e t -> p (e t)"),
                             totals, ALU.subtract))
        do(dve.tensor_tensor(m.place[:].rearrange("p e t -> p (e t)"), m.place[:].rearrange("p e t -> p (e t)"),
                             bank[5][:, 0:E * NT], ALU.add))
        do(dve.tensor_scalar(m.cnt[:], m.incl[:, :, NT - 1], float(P - 1), None, ALU.add))
        do(dve.tensor_scalar(m.tiles_i[:], m.cnt[:], 7, None, ALU.logical_shift_right))
        do(dve.tensor_copy(m.tiles[:], m.tiles_i[:]))
        do(dve.tensor_tensor_scan(m.endt[:], c.fresh[:, 0, 1:1 + E], m.tiles[:], 0.0, ALU.mult, ALU.add))
        do(dve.tensor_tensor(m.base[:], m.endt[:], m.tiles[:], ALU.subtract))
        do(dve.scalar_tensor_tensor(out=m.place[:], in0=m.base[:].unsqueeze(2).to_broadcast([P, E, NT]),
                                    scalar=float(P), in1=m.place[:], op0=ALU.mult, op1=ALU.add))
        for k in range(TOPK):
            do(dve.tensor_tensor(m.eq[:], m.oh[k][:], m.place[:].rearrange("p e t -> p t e"), ALU.mult))
            do(dve.tensor_reduce(m.posf[:, :, k], m.eq[:], AX.X, ALU.add))
        flat = m.posf[:].rearrange("p t k -> p (t k)")
        do(dve.tensor_copy(m.pos[:], flat))
        do(dve.tensor_scalar(m.slot_i[:], m.pos[:], 7, None, ALU.logical_shift_right))
        do(dve.tensor_copy(m.slot[:], m.slot_i[:]))
        do(dve.scalar_tensor_tensor(out=m.lane[:], in0=m.slot[:], scalar=-float(P), in1=flat,
                                    op0=ALU.mult, op1=ALU.add))
        ne = [P, NS, E]
        do(dve.tensor_tensor(m.past[:], c.slot_iota[:, 0:NS].unsqueeze(2).to_broadcast(ne),
                             m.endt[:].unsqueeze(1).to_broadcast(ne), ALU.is_ge))
        do(dve.tensor_reduce(m.wsel[:], m.past[:], AX.X, ALU.add))
        do(dve.tensor_scalar(m.woff[:], m.wsel[:], float(E - 1), float(WE), ALU.min, ALU.mult))

        with dve.Fori(0, NT // 2) as i:
            for p in range(2):
                t = 2 * i + p
                dve.wait_ge(self.hot_used[p], i)
                for k in range(TOPK):
                    at = bass.ds(t * TOPK + k, 1)
                    dve.tensor_scalar(m.hot[p][:, k, :], c.slot_iota[:], m.lane[:, at], None, ALU.is_equal)\
                       .then_inc(self.hot_ready, 1)
                    dve.tensor_scalar(m.vals[p][:, k, 0, :], c.slot_iota[:, 0:NS], m.slot[:, at],
                                      c.t_col[:, bass.ds(t, 1)], ALU.is_equal, ALU.mult).then_inc(self.hot_ready, 1)
                    dve.tensor_scalar(m.vals[p][:, k, 1, :], c.slot_iota[:, 0:NS], m.slot[:, at],
                                      c.p_col[:, 0:1], ALU.is_equal, ALU.mult).then_inc(self.hot_ready, 1)
        dve.wait_ge(self.ids_done, 1)
        do(dve.tensor_scalar(m.idf[:], bank[3][:, 0:NS], float(P), None, ALU.mult))
        dve.tensor_tensor(m.ids[:], m.idf[:], bank[3][:, NS:2 * NS], ALU.add).then_inc(self.ids_ready, 1)

    def combine(self, dve):
        m, c = self.m, self.c
        with dve.Fori(0, NT // 8) as i:
            for p in range(2):
                dve.wait_ge(self.y_back[p], 16 * 4 * TOPK * i + 16 * 4 * TOPK)
                for k in range(TOPK):
                    if k:
                        dve.wait_ge(self.x_done, (4 * TOPK) * (2 * i + p) + 4)
                    for q in range(4):
                        t = 8 * i + (4 * p + q)
                        row = c.x[:, bass.ds(t, 1), :].rearrange("p a c -> p (a c)")
                        add = dve.scalar_tensor_tensor(out=row, in0=m.yg[p][:, q, k, :],
                                                       scalar=m.weight[:, k, bass.ds(t, 1)], in1=row,
                                                       op0=ALU.mult, op1=ALU.add)
                        add.then_inc(self.x_done, 1)
                dve.wait_ge(self.x_done, (4 * TOPK) * (2 * i + p) + 4 * TOPK)
                dve.sem_inc(self.yg_used[p], 4)

    def tensor(self, pe):
        m, c, bank, nc = self.m, self.c, self.c.bank, self.nc
        pe.wait_ge(c.const, c.CONSTS)
        pe.wait_ge(c.beta_ready, 1 + KC)
        for k in range(KC):
            nc.tensor.matmul(bank[6][:, 0:E], c.beta_rep[:, k, :], c.gw[:, k, :], start=k == 0, stop=k == KC - 1)

        def turn(i, p, q):
            r = q % 2
            pe.wait_ge(self.xf_ready, 8 * i + (4 * p + q + 1))
            pe.wait_ge(self.xgt_ready[r], KC * (4 * i + (2 * p + q // 2)))
            for k in range(KC):
                last = nc.tensor.transpose(bank[r][:, k * P:(k + 1) * P], m.xf[p][:, q, k * P:(k + 1) * P], c.ident[:])
            last.then_inc(self.xf_in_psum, 1)

        def score(i, p, q):
            r = q % 2
            pe.wait_ge(self.xgt_ready[r], KC * (4 * i + (2 * p + q // 2)) + KC)
            for k in range(KC):
                last = nc.tensor.matmul(bank[7][:, bass.ds(8 * E * i + (4 * p + q) * E, E)], m.xgt[r][:, k, :],
                                        c.gw[:, k, :], start=k == 0, stop=k == KC - 1)
            last.then_inc(self.xgt_used[r], 1)

        with pe.Fori(0, NT // 8) as i:
            for p in range(2):
                turn(i, p, 0)
                for q in range(1, 4):
                    turn(i, p, q)
                    score(i, p, q - 1)
                pe.wait_ge(self.xf_in_psum, 8 * i + (4 * p + 4))
                pe.sem_inc(self.xf_turned[p], 4)
                score(i, p, 3)
        for r in range(2):
            pe.wait_ge(self.xgt_used[r], NT // 2)
        pe.sem_inc(self.logits_done, 1)

        pe.wait_ge(self.chosen_ready, 1)
        flat = m.chosen[:].rearrange("p e t -> p (e t)")
        nc.tensor.matmul(bank[5][:, 0:E * NT], c.before[:], flat, start=True, stop=True)
        nc.tensor.matmul(bank[4][:, 0:E * NT], c.ones[:], flat, start=True, stop=True).then_inc(self.ranked, 1)

        acc = bank[3][:, 0:2 * NS]
        nc.tensor.matmul(acc, c.zeros[:, 0:P], c.zeros[:], start=True, stop=False)
        with pe.Fori(0, NT // 2) as i:
            for p in range(2):
                pe.wait_ge(self.hot_ready, (3 * TOPK) * (2 * i + (p + 1)))
                for k in range(TOPK):
                    last = nc.tensor.matmul(acc, m.hot[p][:, k, :], m.vals[p][:, k, :, :].rearrange("p a s -> p (a s)"),
                                            start=False, stop=False)
                last.then_inc(self.hot_used[p], 1)
        nc.tensor.matmul(acc, c.zeros[:, 0:P], c.zeros[:], start=False, stop=True).then_inc(self.ids_done, 1)
        pe.wait_ge(self.lo_done, 2 * self.NCH)
        pe.wait_ge(self.ids_ready, 1)
        self.pe_tiles(pe)

    @staticmethod
    def rounds(eng, body):
        for j in range(-1, 4):
            body(j // 2, j % 2, (j >= 0, j >= 1, True, j >= 2))
        with eng.Fori(2, NS // 2 - 1) as i:
            for p in range(2):
                body(i, p, (True, True, True, True))
        for j in range(NS - 2, NS + 2):
            body(j // 2, j % 2, (j < NS, j <= NS, j + 1 < NS, True))

    def pe_tiles(self, pe):
        m, c, bank, nc = self.m, self.c, self.c.bank, self.nc
        xb, hb, tb, yb = bank[0:2], bank[2:4], bank[4:6], bank[6:8]

        def body(i, p, parts):
            j, o = 2 * i + p, 1 - p
            hidden, turn_h, turn_x, out = parts
            if hidden:
                off = pe.value_load(m.woff[0:1, bass.ds(j, 1)], min_val=0, max_val=(E - 1) * WE)
                pe.wait_ge(self.xt_lo, j + 1)
                pe.wait_ge(self.gelu_done, at_least(j - 1))
                for k in range(KC):
                    x = [m.xt[p][s][:, k * P:(k + 1) * P] for s in range(2)]
                    w = [m.w1[s][:, bass.ds(off + k * F, F)] for s in range(2)]
                    last = split_pass(nc, hb[p][:], x[0], x[1], w[0], w[1], k == 0, k == KC - 1)
                last.then_inc(self.h_done, 1)
            if turn_h:
                pe.wait_ge(self.gelu_done, j)
                pe.wait_ge(self.ht_lo, at_least(j - 2))
                for k in range(KF):
                    last = nc.tensor.transpose(tb[o][:, k * P:(k + 1) * P], m.h[o][:, k * P:(k + 1) * P], c.ident[:])
                last.then_inc(self.h_turned, 1)
            if turn_x:
                pe.wait_ge(self.gathered[o], 16 * (i + p) + 16)
                pe.wait_ge(self.xt_lo, at_least(j))
                for k in range(KC):
                    last = nc.tensor.transpose(xb[o][:, k * P:(k + 1) * P], m.xg[o][:, k * P:(k + 1) * P], c.ident[:])
                last.then_inc(self.xg_used[o], 1)
            if out:
                off = pe.value_load(m.woff[0:1, bass.ds(j - 2, 1)], min_val=0, max_val=(E - 1) * WE)
                pe.wait_ge(self.ht_lo, j - 1)
                pe.wait_ge(self.y_ready, at_least(j - 3))
                for k in range(KF):
                    h = [m.ht[p][s][:, k * P:(k + 1) * P] for s in range(2)]
                    w = [m.w2[s][:, bass.ds(off + k * C, C)] for s in range(2)]
                    last = split_pass(nc, yb[p][:, 0:C], h[0], h[1], w[0], w[1], k == 0, k == KF - 1)
                last.then_inc(self.y_done, 1)

        self.rounds(pe, body)

    def act_tiles(self, act):
        m, bank = self.m, self.c.bank
        xb, hb, tb = bank[0:2], bank[2:4], bank[4:6]

        def body(i, p, parts):
            j, o = 2 * i + p, 1 - p
            hidden, turn_h, turn_x, out = parts
            if hidden:
                act.wait_ge(self.h_done, j + 1)
                act.wait_ge(self.h_turned, at_least(j - 1))
                act.activation(m.h[p][:], hb[p][:], ACT.Gelu).then_inc(self.gelu_done, 1)
            if turn_h:
                act.wait_ge(self.h_turned, j)
                act.wait_ge(self.y_done, at_least(j - 2))
                act.activation(m.ht[o][0][:], tb[o][:], ACT.Copy).then_inc(self.ht_hi, 1)
            if turn_x:
                act.wait_ge(self.xg_used[o], i + p + 1)
                act.wait_ge(self.h_done, at_least(j))
                act.activation(m.xt[o][0][:], xb[o][:, 0:C], ACT.Copy).then_inc(self.xt_hi, 1)

        self.rounds(act, body)

    def dve_tiles(self, dve):
        m, bank = self.m, self.c.bank
        xb, tb, yb = bank[0:2], bank[4:6], bank[6:8]

        def body(i, p, parts):
            j, o = 2 * i + p, 1 - p
            hidden, turn_h, turn_x, out = parts
            if turn_h:
                dve.wait_ge(self.ht_hi, j)
                dve.tensor_tensor(m.ht[o][1][:], tb[o][:], m.ht[o][0][:].bitcast(F32), ALU.subtract)\
                   .then_inc(self.ht_lo, 1)
            if turn_x:
                dve.wait_ge(self.xt_hi, j + 2)
                dve.tensor_tensor(m.xt[o][1][:], xb[o][:, 0:C], m.xt[o][0][:].bitcast(F32), ALU.subtract)\
                   .then_inc(self.xt_lo, 1)
            if out:
                dve.wait_ge(self.y_done, j - 1)
                dve.wait_ge(self.y_stored[p], 16 * (i - 1))
                dve.tensor_copy(m.y[p][:], yb[p][:, 0:C]).then_inc(self.y_ready, 1)

        self.rounds(dve, body)




GH = 4
NG = HEADS // GH
SLOTS = HEADS // 2
QK_ROWS = 3 * DK
MAX_ROWS = QK_ROWS + 2
SCALE = (DK ** -0.5, 1.0)
SCORES = P * TB * (TB + 1) // 2
AT_QUERY = [7 * P, 8 * P, 4 * P, 0]
AT_KEY = [0, 4 * P, 8 * P, 7 * P]
HOLDS_SET = ("turn_x", "qk", "v", "max", "attend", "out")
PAIRS = HEADS * DV // P


def steps_of_batch(first, last):
    project = [("turn_x", k) for k in range(KC)] + [("qk", w) for w in range(2)]
    values = [("v", i) for i in range(TB)]
    if first:
        return [("norm",)] + project + values + [("max", 0, h) for h in range(GH)] + [("put_max", 0)]
    order = []
    for g in range(NG):
        ahead = [("max", g + 1, h) for h in range(GH)] if g + 1 < NG else []
        order += ahead[0:2] + [("attend", g, 0)] + ahead[2:4] + [("attend", g, 1)]
        if ahead:
            order += [("put_max", g + 1)]
        elif not last:
            order += project[:-1]
        order += [("attend", g, 2), ("attend", g, 3)]
        if g == NG - 2 and not last:
            order += [("norm",)]
    out = [("out", i) for i in range(TB)]
    if last:
        order += [("flush",)] + out
    else:
        order += project[-1:] + values + [("max", 0, h) for h in range(GH)] + out[:2] + [("put_max", 0)] + out[2:]
    done, behind = [], []
    for step in order:
        if step != ("flush",):
            done.append(step)
        if step[0] in HOLDS_SET or step == ("flush",):
            done += behind
            behind = []
            if step[0] == "attend" and step[2] % 2:
                behind.append(("values", (GH * step[1] + step[2]) // 2))
    assert not behind
    return done


def numbered(order):
    n = 0
    for step in order:
        yield n, step
        n += step[0] in HOLDS_SET


def split_chunks(at, mem):
    n = 0
    for name in ("wq", "wk", "wv", "wo"):
        parts = [w[:].rearrange("p a b -> p (a b)") for w in mem.weights[name]]
        cols = parts[0].shape[1]
        for c in range(0, cols, at.CH):
            yield n, name, slice(c, min(c + at.CH, cols)), parts
            n += 1


class AttentionMemory:
    def __init__(self, nc, ctx):
        def sb(name, shape, dt):
            return ctx.enter_context(nc.sbuf_tensor(name, shape, dt))

        def parts(name, shape):
            return [sb(f"{name}_{x}", shape, F32R) for x in ("hi", "lo")]

        self.wq = parts("wq", [P, KC, HEADS * DK])
        self.wk = parts("wk", [P, KC, HEADS * DK])
        self.wv = parts("wv", [P, KC, HEADS * DV])
        self.wo = parts("wo", [P, HEADS * DV // P, C])
        self.weights = {"wq": self.wq, "wk": self.wk, "wv": self.wv, "wo": self.wo}
        self.q = sb("q_rows", [P, SLOTS, T], F32R)
        self.k = sb("k_rows", [P, SLOTS, T], F32R)
        self.v = sb("v_rows", [P, TB, HEADS * DV], F32)
        self.stats = sb("a_stats", [P, TB, 6], F32)
        self.mv = sb("a_mv", [P, 2, TB], F32)
        self.var = sb("a_var", [P, TB], F32)
        self.rstd = sb("a_rstd", [P, TB], F32)
        self.xn = sb("xn", [P, TB, C], F32)
        self.xt = parts("xnt", [P, KC, T])
        self.staged = [parts(f"qk{i}", [P, T]) for i in range(2)]
        self.p = [sb(f"p_turned{i}", [P, SCORES], F32) for i in range(4)]
        self.negmax = sb("negmax", [P, TB, GH], F32)
        self.sums = sb("sums", [P, TB, GH], F32)
        self.logs = sb("logs", [P, TB, GH], F32)
        self.shift = sb("shift", [P, TB, GH], F32)
        self.maxparts = sb("maxparts", [P, TB, P], F32R)
        self.maxrows = [sb(f"maxrows{i}", [P, T], F32R) for i in range(2)]
        self.ct = parts("ctx", [P, PAIRS, T])
        self.ident_r = sb("ident_r", [P, P], F32R)
        self.ident_b = sb("ident_b", [P, P], BF16)
        self.hide_keys = sb("hide_keys", [P, P], BF16)
        self.hide_turned = sb("hide_turned", [P, P], BF16)


class Attention:

    CH = 1024
    NCHUNKS = 6
    CONSTS = 9

    def __init__(self, core, mem):
        self.c, self.m, self.nc = core, mem, core.nc

        def sem(name):
            return core.sem(f"at_{name}")

        def two(name):
            return [sem(f"{name}{i}") for i in range(2)]

        self.rows_d = [self.nc.dram_tensor(f"{w}_rows_d", [QK_ROWS, HEADS, T], F32, kind="Internal") for w in "qk"]
        self.w_in = two("w_in")
        self.w_hi = sem("w_hi")
        self.w_lo = sem("w_lo")
        self.const = sem("const")
        self.ident_ready = sem("ident_ready")
        self.stats_done = sem("stats_done")
        self.dve_waited = sem("dve_waited")
        self.sp_waited = sem("sp_waited")
        self.mv_done = sem("mv_done")
        self.var_ready = sem("var_ready")
        self.rstd_ready = sem("rstd_ready")
        self.xn_ready = sem("xn_ready")
        self.set_full = sem("set_full")
        self.set_free = two("set_free")
        self.high_ready = sem("high_ready")
        self.staged_out = two("staged_out")
        self.rows_in = [sem(f"rows_in{g}") for g in range(NG)]
        self.rows_read = sem("rows_read")
        self.maxima = sem("maxima")
        self.logs_ready = sem("logs_ready")
        self.shift_ready = sem("shift_ready")
        self.max_high = sem("max_high")
        self.max_split = sem("max_split")
        self.max_turned = sem("max_turned")
        self.max_copied = sem("max_copied")
        self.max_in = [sem(f"max_in{g}") for g in range(NG)]
        self.pv_done = sem("pv_done")
        self.ctx_high = sem("ctx_high")
        self.ctx_split = sem("ctx_split")
        orders = [steps_of_batch(*x) for x in ((True, False), (False, False), (False, True))]
        self.orders = orders
        self.held = [sum(s[0] in HOLDS_SET for s in o) for o in orders]
        assert all(h % 2 == 0 for h in self.held)
        self.total = self.held[0] + (B - 1) * self.held[1] + self.held[2]

    def batches(self, eng, walk):
        start, body, last = self.orders
        n0, nb, _ = self.held
        walk(-1, start, 0)
        with eng.Fori(0, B - 1) as b:
            walk(b, body, b * (nb // 2) + n0 // 2)
        walk(B - 1, last, (B - 1) * (nb // 2) + n0 // 2)

    def wait_all(self, eng):
        for s in range(2):
            eng.wait_ge(self.set_free[s], self.total // 2)

    def wait_set(self, eng, half, n):
        eng.wait_ge(self.set_free[n % 2], half + (n // 2 + 1))

    @staticmethod
    def batch_of(b, g):
        return b + 1 if g == 0 else b

    def pool(self, pool):
        m = self.m
        s = Steps(pool, self.const)
        s.did(pool.memset(m.ident_b[:], 0.0))
        s.did(pool.memset(m.hide_keys[:], 0.0))
        s.did(pool.memset(m.hide_turned[:], 0.0))
        s.settle()
        s.did(pool.memset(m.k[32:64, :, :].bitcast(F32), 1.0))
        s.settle()
        s.did(pool.memset(m.k[96:128, :, :].bitcast(F32), 1.0))
        s.settle()
        s.did(pool.memset(m.maxparts[:].bitcast(F32), 0.0))
        s.settle()
        s.did(pool.affine_select(out=m.ident_b[:], in_=m.ident_b[:], compare_op=ALU.not_equal, fill=1.0,
                                 base=0, pattern=[[-1, P]], channel_multiplier=1))
        s.did(pool.affine_select(out=m.hide_keys[:], in_=m.hide_keys[:], compare_op=ALU.is_ge, fill=NEG,
                                 base=0, pattern=[[-1, P]], channel_multiplier=1))
        s.did(pool.affine_select(out=m.hide_turned[:], in_=m.hide_turned[:], compare_op=ALU.is_ge, fill=NEG,
                                 base=0, pattern=[[1, P]], channel_multiplier=-1))
        assert s.k == self.CONSTS
        with pool.Fori(0, B) as b:
            pool.wait_ge(self.var_ready, b + 1)
            pool.tensor_tensor(m.rstd[:], m.var[:], self.c.minus_half[:, 0:TB], ALU.pow).then_inc(self.rstd_ready, 1)

    def sync(self, sp):
        m = self.m
        for n, name, cut, _ in split_chunks(self, m):
            if n >= 2:
                sp.wait_ge(self.w_lo, n - 1)
            sp.dma_start(m.p[n % 2][:, 0:cut.stop - cut.start],
                         self.c.ins[name].rearrange("p a b -> p (a b)")[:, cut]).then_inc(self.w_in[n % 2], 16)
        sp.wait_ge(self.const, self.CONSTS)

        def store_rows(b, w):
            which = (0, 1, 0) if w == 0 else (0, 0, 1)
            for t in range(2):
                for r in range(3):
                    there = self.rows_d[w][r * DK:(r + 1) * DK, t * SLOTS:(t + 1) * SLOTS, :]
                    sp.dma_start(there.rearrange("p h n -> h p n"), m.staged[t][which[r]][:].bitcast(F32))\
                      .then_inc(self.staged_out[t], 16)

        def load_rows(b):
            for t in range(2):
                sp.wait_ge(self.staged_out[t], 96 * (b + 2))
            for g in range(NG):
                if not isinstance(b, int):
                    sp.wait_ge(self.rows_read, HEADS * b + GH * (g + 1))
                for par in range(2):
                    for w, rows in ((0, m.q), (1, m.k)):
                        src = self.rows_d[w][:].rearrange("r (s two) n -> r s two n", two=2)
                        sp.dma_start(rows[64 * par:64 * par + QK_ROWS, 2 * g:2 * g + 2, :].bitcast(F32),
                                     src[:, 2 * g:2 * g + 2, par, :]).then_inc(self.rows_in[g], 16)

        def walk(b, order, half):
            for n, (kind, *a) in numbered(order):
                if kind == "qk":
                    w = a[0]
                    for g in range(NG):
                        sp.wait_ge(self.rows_in[g], 64 * (b + 1))
                    sp.sem_inc(self.sp_waited, 1)
                    self.wait_set(sp, half, n)
                    store_rows(b, w)
                    if w == 1:
                        load_rows(b)
                elif kind == "put_max":
                    g = a[0]
                    sp.wait_ge(self.max_copied, NG * self.batch_of(b, g) + (g + 1))
                    for h in range(GH):
                        at, slot = 64 * (h % 2) + QK_ROWS, (GH * g + h) // 2
                        sp.dma_start(m.q[at:at + 2, slot, :].bitcast(F32),
                                     m.maxrows[g % 2][2 * h:2 * h + 2, :].bitcast(F32)).then_inc(self.max_in[g], 16)

        self.batches(sp, walk)

    def scalar(self, act):
        m, sets = self.m, self.c.sets
        for n, name, cut, parts in split_chunks(self, m):
            act.wait_ge(self.w_in[n % 2], 16 * (n // 2 + 1))
            act.activation(parts[0][:, cut], m.p[n % 2][:, 0:cut.stop - cut.start], ACT.Copy).then_inc(self.w_hi, 1)
        act.wait_ge(self.w_lo, self.NCHUNKS)

        def walk(b, order, half):
            for n, (kind, *a) in numbered(order):
                s = sets[n % 2]
                if kind in ("turn_x", "qk", "attend"):
                    act.wait_ge(self.set_full, 2 * half + (n + 1))
                if kind == "turn_x":
                    act.activation(m.xt[0][:, a[0], :], s[:, 0:T], ACT.Copy).then_inc(self.high_ready, 1)
                elif kind == "qk":
                    for t in range(2):
                        act.wait_ge(self.staged_out[t], 96 * (b + 1) + 48 * a[0])
                        act.activation(m.staged[t][0][:], s[:, t * T:(t + 1) * T], ACT.Copy, scale=SCALE[a[0]])\
                           .then_inc(self.high_ready, 1)
                elif kind == "attend":
                    g, h = a
                    act.wait_ge(self.pv_done, at_least(PAIRS * b + ((GH * g + h) // 2 - 1))
                                if (GH * g + h) // 2 or isinstance(b, int) else PAIRS * b)
                    act.activation(m.p[h][:], s[:, 0:SCORES], ACT.Exp).then_inc(self.set_free[n % 2], 1)
                elif kind == "max":
                    g, h = a
                    act.wait_ge(self.maxima, HEADS * self.batch_of(b, g) + (GH * g + h + 1))
                    if h == 0:
                        act.wait_ge(self.logs_ready, NG * self.batch_of(b, g) + g)
                    for i in range(TB):
                        block = s[:, AT_QUERY[i]:AT_QUERY[i] + (i + 1) * P]
                        last = act.activation(block, block, ACT.Exp, bias=m.negmax[:, i, h:h + 1],
                                              accum_out=m.sums[:, i, h:h + 1])
                    last.then_inc(self.set_free[n % 2], 1)
                elif kind == "values":
                    act.wait_ge(self.pv_done, PAIRS * b + (a[0] + 1))
                    act.activation(m.ct[0][:, a[0], :], self.c.bank[6][:], ACT.Copy).then_inc(self.ctx_high, 1)
                elif kind == "put_max":
                    g = a[0]
                    now = self.batch_of(b, g)
                    self.wait_maxima(act, order, half, g)
                    act.wait_ge(self.shift_ready, NG * now + g)
                    act.activation(m.logs[:], m.sums[:], ACT.Ln).then_inc(self.logs_ready, 1)
                    act.wait_ge(self.max_turned, NG * now + (g + 1))
                    act.wait_ge(self.max_in[(g - 2) % NG], 64 * now + (64 if g >= 2 else 0))
                    act.activation(m.maxrows[g % 2][0:2 * GH, :], self.c.bank[7][0:2 * GH, 0:T], ACT.Copy)\
                       .then_inc(self.max_copied, 1)

        self.batches(act, walk)

    HIGHS = KC + 4

    def vector(self, dve):
        m, sets, c = self.m, self.c.sets, self.c
        dve.tensor_copy(m.ident_r[:], c.ident[:]).then_inc(self.ident_ready, 1)
        for n, name, cut, parts in split_chunks(self, m):
            dve.wait_ge(self.w_hi, n + 1)
            dve.tensor_tensor(parts[1][:, cut], m.p[n % 2][:, 0:cut.stop - cut.start],
                              parts[0][:, cut].bitcast(F32), ALU.subtract).then_inc(self.w_lo, 1)
        dve.wait_ge(self.const, self.CONSTS)

        def highs(b, k):
            dve.wait_ge(self.high_ready, self.HIGHS * b + (self.HIGHS + k + 1))

        def walk(b, order, half):
            k = 0
            for n, (kind, *a) in numbered(order):
                s, free = sets[n % 2], self.set_free[n % 2]
                if kind == "norm":
                    def row(i):
                        return c.x[:, TB * (b + 1) + i, :] if isinstance(b, int) else \
                            c.x[:, bass.ds(TB * b + (TB + i), 1), :].rearrange("p a c -> p (a c)")
                    for i in range(TB):
                        dve.bn_stats(m.stats[:, i, :], row(i)).then_inc(self.stats_done, 1)
                    dve.wait_ge(self.stats_done, TB * (b + 2))
                    dve.sem_inc(self.dve_waited, 1)
                    for i in range(TB):
                        dve.bn_aggr(m.mv[:, :, i], m.stats[:, i, :]).then_inc(self.mv_done, 1)
                    dve.wait_ge(self.mv_done, TB * (b + 2))
                    dve.tensor_scalar(m.var[:], m.mv[:, 1, :], EPS, None, ALU.add).then_inc(self.var_ready, 1)
                    dve.wait_ge(self.rstd_ready, b + 2)
                    for i in range(TB):
                        dve.tensor_scalar(m.xn[:, i, :], row(i), m.mv[:, 0, i:i + 1], m.rstd[:, i:i + 1],
                                          ALU.subtract, ALU.mult).then_inc(self.xn_ready, 1)
                elif kind == "turn_x":
                    highs(b, k)
                    k += 1
                    dve.tensor_tensor(m.xt[1][:, a[0], :], s[:, 0:T], m.xt[0][:, a[0], :].bitcast(F32),
                                      ALU.subtract).then_inc(free, 1)
                elif kind == "qk":
                    for t in range(2):
                        highs(b, k)
                        k += 1
                        low = dve.scalar_tensor_tensor(out=m.staged[t][1][:], in0=s[:, t * T:(t + 1) * T],
                                                       scalar=SCALE[a[0]], in1=m.staged[t][0][:].bitcast(F32),
                                                       op0=ALU.mult, op1=ALU.subtract)
                    low.then_inc(free, 1)
                elif kind == "max":
                    g, h = a
                    dve.wait_ge(self.set_full, 2 * half + (n + 1))
                    if h == 0:
                        dve.wait_ge(self.max_split, NG * self.batch_of(b, g) + g)
                    for i in range(TB):
                        last = dve.tensor_reduce(m.negmax[:, i, h:h + 1], s[:, AT_QUERY[i]:AT_QUERY[i] + (i + 1) * P],
                                                 AX.X, ALU.max, negate=True)
                    last.then_inc(self.maxima, 1)
                elif kind == "put_max":
                    g = a[0]
                    number = NG * self.batch_of(b, g) + g
                    dve.wait_ge(self.logs_ready, number + 1)
                    dve.wait_ge(self.max_high, number)
                    dve.tensor_tensor(m.shift[:], m.negmax[:], m.logs[:], ALU.subtract).then_inc(self.shift_ready, 1)
                    dve.wait_ge(self.max_turned, number)
                    dve.wait_ge(self.shift_ready, number + 1)
                    dve.tensor_copy(m.maxparts[:, :, 0:2 * GH:2], m.shift[:]).then_inc(self.max_high, 1)
                    dve.wait_ge(self.max_high, number + 1)
                    dve.tensor_tensor(m.maxparts[:, :, 1:2 * GH:2], m.shift[:],
                                      m.maxparts[:, :, 0:2 * GH:2].bitcast(F32), ALU.subtract)\
                       .then_inc(self.max_split, 1)
                elif kind == "v":
                    dve.wait_ge(self.set_full, 2 * half + (n + 1))
                    dve.tensor_copy(m.v[:, a[0], :], s[:, 0:HEADS * DV]).then_inc(free, 1)
                elif kind == "values":
                    dve.wait_ge(self.ctx_high, PAIRS * b + (a[0] + 1))
                    dve.tensor_tensor(m.ct[1][:, a[0], :], self.c.bank[6][:], m.ct[0][:, a[0], :].bitcast(F32),
                                      ALU.subtract).then_inc(self.ctx_split, 1)
                elif kind == "out":
                    dve.wait_ge(self.set_full, 2 * half + (n + 1))
                    row = c.x[:, TB * b + a[0], :] if isinstance(b, int) else \
                        c.x[:, bass.ds(TB * b + a[0], 1), :].rearrange("p a c -> p (a c)")
                    dve.tensor_tensor(row, row, s[:, 0:C], ALU.add).then_inc(free, 1)

        self.batches(dve, walk)
        self.wait_all(dve)

    def wait_maxima(self, eng, order, half, g):
        n = next(n for n, step in numbered(order) if step == ("max", g, GH - 1))
        self.wait_set(eng, half, n)

    def tensor(self, pe):
        m, sets, c, nc = self.m, self.c.sets, self.c, self.nc
        pe.wait_ge(self.w_lo, self.NCHUNKS)
        pe.wait_ge(self.const, self.CONSTS)
        pe.wait_ge(self.ident_ready, 1)

        def scores(s, stationary, moving, rows, at, starts, length, hide):
            blocks = sorted(range(TB), key=lambda i: at[i])
            opened = set()
            for i in blocks:
                bank = at[i] // 512
                start, size = starts(i), length(i)
                last = nc.tensor.matmul(s[:, at[i]:at[i] + size], stationary[:, i * P:(i + 1) * P],
                                        moving[:, start:start + size], start=bank not in opened, stop=False,
                                        skip_group_check=True)
                opened.add(bank)
            read = last
            for i in blocks:
                diagonal = at[i] + (i * P - starts(i))
                last = nc.tensor.matmul(s[:, diagonal:diagonal + P], m.ident_b[:], hide[:], start=False, stop=True,
                                        skip_group_check=True)
            return read, last

        def head(x, h, rows):
            at = 64 * (h % 2)
            return x[at:at + rows, h // 2, :]

        def walk(b, order, half):
            where = {step: n for n, step in numbered(order)}
            for n, (kind, *a) in numbered(order):
                s = sets[n % 2]
                if kind in HOLDS_SET:
                    pe.wait_ge(self.set_free[n % 2], half + n // 2)
                if kind == "turn_x":
                    pe.wait_ge(self.xn_ready, TB * (b + 2))
                    k = a[0]
                    for i in range(TB):
                        last = nc.tensor.transpose(s[:, i * P:(i + 1) * P], m.xn[:, i, k * P:(k + 1) * P], c.ident[:])
                elif kind == "qk":
                    if a[0] == 0:
                        for k in range(KC):
                            self.wait_set(pe, half, where["turn_x", k])
                    w = (m.wq, m.wk)[a[0]]
                    for t in range(2):
                        for k in range(KC):
                            last = split_pass(nc, s[:, t * T:(t + 1) * T], w[0][:, k, t * P:(t + 1) * P],
                                              w[1][:, k, t * P:(t + 1) * P], m.xt[0][:, k, :], m.xt[1][:, k, :],
                                              k == 0, k == KC - 1)
                elif kind == "v":
                    i = a[0]
                    for half_v in range(2):
                        cut = slice(half_v * 512, (half_v + 1) * 512)
                        for k in range(KC):
                            last = split_pass(nc, s[:, cut], m.xt[0][:, k, i * P:(i + 1) * P],
                                              m.xt[1][:, k, i * P:(i + 1) * P], m.wv[0][:, k, cut], m.wv[1][:, k, cut],
                                              k == 0, k == KC - 1)
                elif kind == "max":
                    g, h = a
                    if h == 0:
                        pe.wait_ge(self.rows_in[g], 64 * self.batch_of(b, g) + 64)
                    _, last = scores(s, head(m.q, GH * g + h, QK_ROWS), head(m.k, GH * g + h, QK_ROWS), QK_ROWS,
                                     AT_QUERY, lambda i: 0, lambda i: (i + 1) * P, m.hide_keys)
                elif kind == "put_max":
                    number = NG * self.batch_of(b, a[0]) + a[0]
                    pe.wait_ge(self.max_split, number + 1)
                    pe.wait_ge(self.max_copied, number)
                    for i in range(TB):
                        turned = nc.tensor.matmul(c.bank[7][:, i * P:(i + 1) * P], m.maxparts[:, i, :], m.ident_r[:],
                                                  start=True, stop=True)
                    turned.then_inc(self.max_turned, 1)
                elif kind == "attend":
                    g, h = a
                    if h == 0:
                        pe.wait_ge(self.max_in[g], 64 * b + 64)
                    read, last = scores(s, head(m.k, GH * g + h, MAX_ROWS), head(m.q, GH * g + h, MAX_ROWS), MAX_ROWS,
                                        AT_KEY, lambda i: i * P, lambda i: (TB - i) * P, m.hide_turned)
                    read.then_inc(self.rows_read, 1)
                elif kind == "values":
                    pair = a[0]
                    g, h = pair // (GH // 2), pair % (GH // 2) * 2
                    for k in range(2):
                        self.wait_set(pe, half, where["attend", g, h + k])
                    pe.wait_ge(self.ctx_split, PAIRS * b + pair)
                    for j in range(TB):
                        for k in range(2):
                            at = (2 * pair + k) * DV
                            pv = nc.tensor.matmul(c.bank[6][k * DV:(k + 1) * DV, j * P:T], m.v[:, j, at:at + DV],
                                                  m.p[h + k][:, AT_KEY[j]:AT_KEY[j] + (TB - j) * P],
                                                  start=j == 0, stop=j == TB - 1)
                    pv.then_inc(self.pv_done, 1)
                elif kind == "out":
                    i = a[0]
                    pe.wait_ge(self.ctx_split, PAIRS * (b + 1))
                    cut = slice(i * P, (i + 1) * P)
                    for k in range(PAIRS):
                        last = split_pass(nc, s[:, 0:C], m.ct[0][:, k, cut], m.ct[1][:, k, cut], m.wo[0][:, k, :],
                                          m.wo[1][:, k, :], k == 0, k == PAIRS - 1)
                if kind in HOLDS_SET:
                    last.then_inc(self.set_full, 1)

        self.batches(pe, walk)


def layout(inputs, np):
    a = {k: np.ascontiguousarray(np.asarray(v)) for k, v in inputs.items()}

    def rows(w, k):
        return np.ascontiguousarray(w.reshape(k, P, -1).transpose(1, 0, 2))

    w1 = a["L0_ffn_w1"].transpose(0, 2, 1).reshape(E, KC, P, F).transpose(2, 0, 1, 3)
    w2 = a["L0_ffn_w2"].transpose(0, 2, 1).reshape(E, KF, P, C).transpose(2, 0, 1, 3)
    return {
        "x": a["L0_attn_x"].reshape(N, C),
        "gate": rows(a["L0_ffn_gate_w"].T, KC),
        "gamma": np.ascontiguousarray(a["L0_ffn_ln_gamma"].reshape(KC, P).T),
        "beta": np.ascontiguousarray(a["L0_ffn_ln_beta"].reshape(KC, P).T),
        "w1": np.ascontiguousarray(w1).reshape(P, E * WE),
        "w2": np.ascontiguousarray(w2).reshape(P, E * WE),
        "wq": rows(a["L0_attn_Wq"], KC),
        "wk": rows(a["L0_attn_Wk"], KC),
        "wv": rows(a["L0_attn_Wv"], KC),
        "wo": rows(a["L0_attn_Wo"], HEADS * DV // P),
    }


def build(nc, ins, out):
    with ExitStack() as ctx:
        core = Core(nc, ctx, ins)
        with ExitStack() as scope:
            moe_memory = MoeMemory(nc, scope)
        with ExitStack() as scope:
            attention_memory = AttentionMemory(nc, scope)
        first = Moe(core, moe_memory, "moe1")
        attention = Attention(core, attention_memory)
        second = Moe(core, moe_memory, "moe2")
        stored = core.sem("out_stored")
        block = ctx.enter_context(nc.Block())

        def after_first(eng):
            eng.wait_ge(first.x_done, NT * TOPK)

        @block.sync
        def _(sp):
            core.sync(sp)
            first.sync(sp)
            after_first(sp)
            attention.sync(sp)
            attention.wait_all(sp)
            second.sync(sp)
            rows, there = core.x, out.rearrange("(t p) c -> p t c", p=P)
            with sp.Fori(0, NT // 4) as g:
                sp.wait_ge(core.x_rows, 32)
                sp.wait_ge(second.x_done, 4 * TOPK * g + 4 * TOPK)
                sp.dma_start(there[:, bass.ds(g * 4, 4), :], rows[:, bass.ds(g * 4, 4), :]).then_inc(stored, 16)
            sp.wait_ge(stored, 16 * (NT // 4))

        @block.gpsimd
        def _(pool):
            core.pool(pool)
            first.pool(pool)
            after_first(pool)
            attention.pool(pool)
            attention.wait_all(pool)
            second.pool(pool)

        @block.scalar
        def _(act):
            first.scalar(act)
            after_first(act)
            attention.scalar(act)
            attention.wait_all(act)
            second.scalar(act)

        @block.vector
        def _(dve):
            core.vector(dve)
            dve.wait_ge(core.x_rows, 32)
            first.vector(dve)
            after_first(dve)
            attention.vector(dve)
            second.vector(dve)

        @block.tensor
        def _(pe):
            first.tensor(pe)
            after_first(pe)
            attention.tensor(pe)
            attention.wait_all(pe)
            second.tensor(pe)


def kernel(**inputs):
    import numpy as np
    import concourse.bacc as bacc
    from concourse.bass_utils import run_bass_kernel_spmd

    arrays = {f"in_{name}": a for name, a in layout(inputs, np).items()}
    nc = bacc.Bacc("TRN2", target_bir_lowering=False, num_devices=1)
    ins = {name[3:]: nc.dram_tensor(name, a.shape, mybir.dt.from_np(a.dtype), kind="ExternalInput").ap()
           for name, a in arrays.items()}
    out = nc.dram_tensor("out_rows", [N, C], F32, kind="ExternalOutput").ap()
    build(nc, ins, out)
    r = run_bass_kernel_spmd(nc, [arrays], core_ids=[0])
    return r.results[0]["out_rows"].reshape(B, T, C)
```

```python
from contextlib import ExitStack

import concourse.bass as bass
from concourse import mybir

ALU = mybir.AluOpType
ACT = mybir.ActivationFunctionType
AX = mybir.AxisListType
F32 = mybir.dt.float32
F32R = mybir.dt.float32r
BF16 = mybir.dt.bfloat16
I32 = mybir.dt.int32

P = 128
B, T, C = 8, 512, 256
N = B * T
NT = N // P
TB = T // P
KC = C // P
E, TOPK, F = 8, 2, 512
KF = F // P
NS = N * TOPK // P + E
EPS = 1e-5
WE = KC * F
assert WE == KF * C
HEADS, DK, DV = 16, 16, 64
NEG = -3.0e38
STAGED = 3


class Steps:

    def __init__(self, eng, sem):
        self.eng, self.sem, self.base, self.k = eng, sem, 0, 0

    def did(self, ins):
        ins.then_inc(self.sem, 1)
        self.k += 1

    def settle(self):
        self.eng.wait_ge(self.sem, self.base + self.k)

    def loop(self, start, end, per, body):
        first = self.base + self.k
        with self.eng.Fori(start, end) as i:
            self.base, self.k = i * per + (first - start * per), 0
            body(i)
            assert self.k == per, (self.k, per)
        self.base, self.k = first + (end - start) * per, 0


def split_pass(nc, out, hi, lo, rhi, rlo, start, stop):
    nc.tensor.matmul(out, lo, rhi, start=start, stop=False)
    nc.tensor.matmul(out, hi, rlo, start=False, stop=False)
    return nc.tensor.matmul(out, hi, rhi, start=False, stop=stop)


def at_least(n):
    return max(n, 0) if isinstance(n, int) else n


class Core:

    QUARTERS = 4

    def __init__(self, nc, ctx, ins):
        self.nc, self.ins = nc, ins

        def sb(name, shape, dt):
            return ctx.enter_context(nc.sbuf_tensor(name, shape, dt))

        def sem(name):
            return ctx.enter_context(nc.semaphore(name))

        self.sem = sem
        psum = ctx.enter_context(nc.psum_tensor("psum", [P, 8, 512], F32))
        self.bank = [psum[:, i, :] for i in range(8)]
        self.sets = [psum[:, 3 * i:3 * i + 3, :].rearrange("p a b -> p (a b)") for i in range(2)]
        self.x = sb("x_rows", [P, NT, C], F32)
        self.ident = sb("ident", [P, P], F32)
        self.before = sb("before", [P, P], BF16)
        self.ones = sb("ones", [P, P], BF16)
        self.zeros = sb("zeros", [P, P], BF16)
        self.slot_iota = sb("slot_iota", [P, P], BF16)
        self.e_iota = sb("e_iota", [P, E], F32)
        self.token = sb("token", [P, NT], F32)
        self.fresh = sb("fresh", [P, E, NT], F32)
        self.gw = sb("gw", [P, KC, E], F32)
        self.gamma = sb("gamma", [P, KC], F32)
        self.beta = sb("beta", [P, KC], F32)
        self.beta_rep = sb("beta_rep", [P, KC, P], F32)
        self.minus_half = sb("minus_half", [P, NT], F32)
        self.pos = sb("pos", [P, NT * TOPK], I32)
        self.weight = sb("weight", [P, TOPK, NT], F32)
        self.y_pair = sb("y_pair", [P, 2, TOPK, C], F32)
        self.y_ids = sb("y_ids", [P, 2 * TOPK], I32)
        self.x_rows = [sem(f"x_loaded{q}") for q in range(self.QUARTERS)]
        self.small = sem("small_loaded")
        self.const = sem("const_ready")
        self.beta_ready = sem("beta_ready")
        self.waited = sem("waited")

    CONSTS = 11

    def sync(self, sp):
        sp.dma_start(self.gw[:], self.ins["gate"]).then_inc(self.small, 16)
        sp.dma_start(self.gamma[:], self.ins["gamma"]).then_inc(self.small, 16)
        sp.dma_start(self.beta[:], self.ins["beta"]).then_inc(self.small, 16)
        x = self.ins["x"].rearrange("(t p) c -> p t c", p=P)
        for q in range(self.QUARTERS):
            cut = slice(q * NT // self.QUARTERS, (q + 1) * NT // self.QUARTERS)
            sp.dma_start(self.x[:, cut, :], x[:, cut, :]).then_inc(self.x_rows[q], 16)

    def pool(self, pool):
        c = Steps(pool, self.const)
        c.did(pool.memset(self.minus_half[:], -0.5))
        c.did(pool.memset(self.ident[:], 0.0))
        c.did(pool.memset(self.before[:], 1.0))
        c.did(pool.memset(self.ones[:], 1.0))
        c.did(pool.memset(self.zeros[:], 0.0))
        c.did(pool.memset(self.fresh[:], 1.0))
        c.did(pool.iota(self.slot_iota[:], pattern=[[1, P]], base=0, channel_multiplier=0,
                        allow_small_or_imprecise_dtypes=True))
        c.did(pool.iota(self.e_iota[:], pattern=[[1, E]], base=-E, channel_multiplier=0,
                        allow_small_or_imprecise_dtypes=True))
        c.did(pool.iota(self.token[:], pattern=[[P, NT]], base=0, channel_multiplier=1,
                        allow_small_or_imprecise_dtypes=True))
        c.settle()
        c.did(pool.affine_select(out=self.ident[:], in_=self.ident[:], compare_op=ALU.not_equal, fill=1.0,
                                 base=0, pattern=[[-1, P]], channel_multiplier=1))
        c.did(pool.affine_select(out=self.before[:], in_=self.before[:], compare_op=ALU.is_gt, fill=0.0,
                                 base=0, pattern=[[1, P]], channel_multiplier=-1))
        c.settle()
        assert c.k == self.CONSTS

    def vector(self, dve):
        dve.wait_ge(self.const, self.CONSTS)
        dve.wait_ge(self.small, 48)
        dve.memset(self.fresh[:, :, 0:1], 0.0).then_inc(self.beta_ready, 1)
        for k in range(KC):
            dve.tensor_scalar(self.beta_rep[:, k, :], self.ident[:], 0.0, self.beta[:, k:k + 1],
                              ALU.mult, ALU.add).then_inc(self.beta_ready, 1)
        dve.wait_ge(self.beta_ready, 1 + KC)


class MoeMemory:

    def __init__(self, nc, ctx):
        def sb(name, shape, dt):
            return ctx.enter_context(nc.sbuf_tensor(name, shape, dt))

        with nc.sbuf_tensor("y_gathered", [P, 2, 4, TOPK, C], F32) as yg:
            self.yg = [yg[:, i, :, :, :] for i in range(2)]
        self.w1 = [sb(f"w1_{x}", [P, E * WE], F32R) for x in ("hi", "lo")]
        self.w2 = [sb(f"w2_{x}", [P, E * WE], F32R) for x in ("hi", "lo")]
        self.staged = [sb(f"staged{i}", [P, 1024], F32) for i in range(STAGED)]
        self.woff = sb("woff", [P, NS], I32)
        self.ids = sb("ids", [P, NS], I32)
        self.idc = [sb(f"idc{i}", [P, 4 * TOPK], I32) for i in range(2)]
        te = [P, NT, E]
        with ExitStack() as ctx:
            self.stats = sb("stats", [P, NT // Core.QUARTERS, 6], F32)
            self.mv = sb("mv", [P, 2, NT], F32)
            self.var = sb("var_eps", [P, NT], F32)
            self.rstd = sb("rstd", [P, NT], F32)
            self.rr = sb("rr", [P, NT], F32)
            self.var2 = sb("var2_eps", [P, NT], F32)
            self.rstd2 = sb("rstd2", [P, NT], F32)
            self.xf = [sb(f"xf{i}", [P, 4, C], F32) for i in range(2)]
            self.xgt = [sb(f"xgt{i}", [P, KC, P], F32) for i in range(4)]
            self.logits = sb("logits", te, F32)
            self.ex = sb("ex", te, F32)
            self.eq = sb("eq", te, F32)
            self.oh = [sb(f"oh{i}", te, F32) for i in range(2)]
            self.row = sb("row", [P, NT], F32)
            self.best = [sb(f"best{i}", [P, NT], F32) for i in range(2)]
            self.rinv = sb("rinv", [P, NT], F32)
            self.chosen = sb("chosen", [P, E, NT], BF16)
            self.incl = sb("incl", [P, E, NT], F32)
            self.place = sb("place", [P, E, NT], F32)
            self.cnt = sb("cnt", [P, E], I32)
            self.tiles_i = sb("tiles_i", [P, E], I32)
            self.tiles = sb("tiles", [P, E], F32)
            self.endt = sb("endt", [P, E], F32)
            self.base = sb("base", [P, E], F32)
            self.posf = sb("posf", [P, NT, TOPK], F32)
            self.slot_i = sb("slot_i", [P, NT * TOPK], I32)
            self.slot = sb("slot", [P, NT * TOPK], F32)
            self.lane = sb("lane", [P, NT * TOPK], F32)
            self.past = sb("past", [P, NS, E], BF16)
            self.wsel = sb("wsel", [P, NS], F32)
            self.hot = [sb(f"hot{i}", [P, TOPK, P], F32R) for i in range(2)]
            self.vals = [sb(f"vals{i}", [P, TOPK, NS], F32R) for i in range(2)]
        with ExitStack() as ctx:
            self.idb = [sb(f"idb{i}", [P, 1], I32) for i in range(2)]
            self.xg = [sb(f"xg{i}", [P, C], F32) for i in range(2)]
            self.xt = [[sb(f"xt{i}_{x}", [P, C], F32R) for x in ("hi", "lo")] for i in range(2)]
            self.h = [sb(f"h{i}", [P, F], F32) for i in range(2)]
            self.ht = [[sb(f"ht{i}_{x}", [P, F], F32R) for x in ("hi", "lo")] for i in range(2)]
            self.y = [sb(f"y{i}", [P, C], F32) for i in range(2)]


class Moe:

    CH = 1024
    NCH = E * WE // CH
    EARLY = 3

    def __init__(self, core, mem, tag):
        nc, self.c, self.m = core.nc, core, mem
        self.nc = nc
        self.xf_d = nc.dram_tensor(f"{tag}_xf", [N, C], F32, kind="Internal")
        self.y_d = nc.dram_tensor(f"{tag}_y", [NS * P, C], F32, kind="Internal")

        def sem(name):
            return core.sem(f"{tag}_{name}")

        def two(name):
            return [sem(f"{name}{i}") for i in range(2)]

        self.staged_in = [sem(f"staged_in{i}") for i in range(STAGED)]
        self.hi_done = sem("hi_done")
        self.lo_done = sem("lo_done")
        self.dve_step = sem("dve_step")
        self.var_ready = sem("var_ready")
        self.rstd_ready = sem("rstd_ready")
        self.xf_ready = sem("xf_ready")
        self.xf_stored = two("xf_stored")
        self.xf_in_psum = sem("xf_in_psum")
        self.xgt_ready = sem("xgt_ready")
        self.scored = sem("scored")
        self.logits_done = sem("logits_done")
        self.shifted = sem("shifted")
        self.ex_ready = sem("ex_ready")
        self.chosen_ready = sem("chosen_ready")
        self.ranked = sem("ranked")
        self.hot_ready = sem("hot_ready")
        self.hot_used = two("hot_used")
        self.ids_done = sem("ids_done")
        self.ids_ready = sem("ids_ready")
        self.idb_ready = sem("idb_ready")
        self.gathered = two("gathered")
        self.xg_used = two("xg_used")
        self.xt_hi = sem("xt_hi")
        self.xt_lo = sem("xt_lo")
        self.h_done = sem("h_done")
        self.gelu_done = sem("gelu_done")
        self.h_turned = sem("h_turned")
        self.ht_hi = sem("ht_hi")
        self.ht_lo = sem("ht_lo")
        self.y_done = sem("y_done")
        self.y_ready = sem("y_ready")
        self.y_stored = two("y_stored")
        self.idc_ready = sem("idc_ready")
        self.y_back = two("y_back")
        self.yg_used = two("yg_used")
        self.x_done = sem("x_done")

    def sync(self, sp):
        rows = self.xf_d[:].rearrange("(t p) c -> p t c", p=P)
        with sp.Fori(0, NT // 8) as i:
            for p in range(2):
                sp.wait_ge(self.c.small, 48)
                sp.wait_ge(self.xf_ready, 8 * i + 4 * (p + 1))
                sp.dma_start(rows[:, bass.ds(8 * i + 4 * p, 4), :], self.m.xf[p][:]).then_inc(self.xf_stored[p], 16)
        self.sync_y(sp)

    def sync_y(self, sp):
        m = self.m
        with sp.Fori(0, NS // 2) as i:
            for p in range(2):
                sp.wait_ge(self.c.small, 48)
                sp.wait_ge(self.y_ready, 2 * i + (p + 1))
                sp.dma_start(self.y_d[bass.ds(i * (2 * P) + p * P, P), :], m.y[p][:])\
                  .then_inc(self.y_stored[p], 16)

    def act_split(self, act):
        m = self.m

        def load(n):
            src, c = (self.c.ins["w1"], n) if n < self.NCH else (self.c.ins["w2"], n - self.NCH)
            act.dma_start(m.staged[n % STAGED][:], src[:, c * self.CH:(c + 1) * self.CH])\
               .then_inc(self.staged_in[n % STAGED], 16)

        for n in range(STAGED - 1):
            load(n)
        for n in range(2 * self.NCH):
            if n + STAGED - 1 < 2 * self.NCH:
                if n:
                    act.wait_ge(self.lo_done, n)
                load(n + STAGED - 1)
            w, c = (m.w1, n) if n < self.NCH else (m.w2, n - self.NCH)
            act.wait_ge(self.staged_in[n % STAGED], 16 * (n // STAGED + 1))
            act.activation(w[0][:, c * self.CH:(c + 1) * self.CH], m.staged[n % STAGED][:], ACT.Copy)\
               .then_inc(self.hi_done, 1)

    def scalar(self, act):
        self.act_split(act)
        act.wait_ge(self.shifted, 1)
        act.activation(self.m.ex[:], self.m.logits[:], ACT.Exp).then_inc(self.ex_ready, 1)
        self.act_tiles(act)

    def pool(self, pool):
        m, c = self.m, self.c

        def low_parts(chunks):
            for n in chunks:
                w, k = (m.w1, n) if n < self.NCH else (m.w2, n - self.NCH)
                cut = slice(k * self.CH, (k + 1) * self.CH)
                pool.wait_ge(self.hi_done, n + 1)
                pool.tensor_tensor(w[1][:, cut], m.staged[n % STAGED][:], w[0][:, cut].bitcast(F32), ALU.subtract)\
                    .then_inc(self.lo_done, 1)

        low_parts(range(self.EARLY))
        pool.wait_ge(self.var_ready, 1)
        pool.tensor_tensor(m.rstd[:], m.var[:], c.minus_half[:], ALU.pow).then_inc(self.rstd_ready, 1)
        pool.wait_ge(self.var_ready, 2)
        pool.tensor_tensor(m.rstd2[:], m.var2[:], c.minus_half[:], ALU.pow).then_inc(self.rstd_ready, 1)
        low_parts(range(self.EARLY, 2 * self.NCH))
        for p in range(2):
            pool.wait_ge(self.xf_stored[p], 16 * (NT // 8))
        pool.wait_ge(self.ids_ready, 1)
        with pool.Fori(0, NS // 2) as i:
            for p in range(2):
                pool.wait_ge(self.xg_used[p], i)
                pool.tensor_copy(m.idb[p][:], m.ids[:, bass.ds(2 * i + p, 1)]).then_inc(self.idb_ready, 1)
                pool.wait_ge(self.idb_ready, 2 * i + (p + 1))
                pool.sem_inc(self.c.waited, 1)
                pool.indirect_dma_start(out=m.xg[p][:], out_offset=None, in_=self.xf_d[:],
                                        in_offset=bass.IndirectOffsetOnAxis(ap=m.idb[p][:, 0:1], axis=0))\
                    .then_inc(self.gathered[p], 16)

    def wait_stored(self, eng):
        for p in range(2):
            eng.wait_ge(self.y_stored[p], 16 * (NS // 2))

    def gather_results(self, pool):
        m, c = self.m, self.c
        self.wait_stored(pool)
        with pool.Fori(0, NT // 8) as i:
            for p in range(2):
                g = 2 * i + p
                pool.wait_ge(self.yg_used[p], 4 * i)
                pool.tensor_copy(m.idc[p][:], c.pos[:, bass.ds(g * (4 * TOPK), 4 * TOPK)])\
                    .then_inc(self.idc_ready, 1)
                pool.wait_ge(self.idc_ready, g + 1)
                pool.sem_inc(self.c.waited, 1)
                for q in range(4 * TOPK):
                    pool.indirect_dma_start(out=m.yg[p][:, q // TOPK, q % TOPK, :], out_offset=None,
                                            in_=self.y_d[:],
                                            in_offset=bass.IndirectOffsetOnAxis(ap=m.idc[p][:, q:q + 1], axis=0))\
                        .then_inc(self.y_back[p], 16)

    def vector(self, dve):
        m, c, bank = self.m, self.c, self.c.bank
        s = Steps(dve, self.dve_step)
        quarter = NT // c.QUARTERS
        for q in range(c.QUARTERS):
            dve.wait_ge(c.x_rows[q], 16)
            s.settle()
            for t in range(quarter):
                s.did(dve.bn_stats(m.stats[:, t, :], c.x[:, q * quarter + t, :]))
            s.settle()
            for t in range(quarter):
                s.did(dve.bn_aggr(m.mv[:, :, q * quarter + t], m.stats[:, t, :]))
        s.settle()
        dve.tensor_scalar(m.var[:], m.mv[:, 1, :], EPS, None, ALU.add).then_inc(self.var_ready, 1)
        dve.wait_ge(self.rstd_ready, 1)
        s.did(dve.tensor_tensor(m.rr[:], m.rstd[:], m.rstd[:], ALU.mult))
        s.settle()
        s.did(dve.tensor_tensor(m.rr[:], m.rr[:], m.mv[:, 1, :], ALU.mult))
        s.settle()
        dve.tensor_scalar(m.var2[:], m.rr[:], EPS, None, ALU.add).then_inc(self.var_ready, 1)
        with dve.Fori(0, NT // 8) as i:
            for p in range(2):
                dve.wait_ge(self.xf_stored[p], 16 * i)
                for q in range(4):
                    t = 8 * i + (4 * p + q)
                    dve.tensor_scalar(m.xf[p][:, q, :], c.x[:, bass.ds(t, 1), :].rearrange("p a c -> p (a c)"),
                                      m.mv[:, 0, bass.ds(t, 1)], m.rstd[:, bass.ds(t, 1)],
                                      ALU.subtract, ALU.mult).then_inc(self.xf_ready, 1)
                for q in range(4):
                    number = 8 * i + (4 * p + q)
                    dve.wait_ge(self.xf_in_psum, number + 1)
                    if p:
                        dve.wait_ge(self.scored, number - 3)
                    else:
                        dve.wait_ge(self.scored, 8 * i)
                    for k in range(KC):
                        dve.tensor_scalar(m.xgt[q][:, k, :], bank[q][:, k * P:(k + 1) * P], c.gamma[:, k:k + 1],
                                          None, ALU.mult).then_inc(self.xgt_ready, 1)
        self.route(dve, s)
        self.dve_tiles(dve)

    def route(self, dve, s):
        m, c, bank = self.m, self.c, self.c.bank
        te = [P, NT, E]

        def do(ins):
            s.did(ins)
            s.settle()

        def tile_wide(ap):
            return ap[:].unsqueeze(2).to_broadcast(te)

        experts = c.e_iota[:].unsqueeze(1).to_broadcast(te)
        dve.wait_ge(self.logits_done, 1)
        dve.wait_ge(self.rstd_ready, 2)
        do(dve.tensor_tensor(m.logits[:], bank[7][:, 0:NT * E].rearrange("p (t e) -> p t e", e=E),
                             tile_wide(m.rstd2), ALU.mult))
        do(dve.tensor_tensor(m.logits[:], m.logits[:], bank[6][:, 0:E].unsqueeze(1).to_broadcast(te), ALU.add))
        do(dve.tensor_reduce(m.row[:], m.logits[:], AX.X, ALU.max))
        s.did(dve.tensor_tensor(m.logits[:], m.logits[:], tile_wide(m.row), ALU.subtract))
        s.settle()
        dve.sem_inc(self.shifted, 1)
        dve.wait_ge(self.ex_ready, 1)
        do(dve.tensor_reduce(m.row[:], m.ex[:], AX.X, ALU.add))
        do(dve.reciprocal(m.rinv[:], m.row[:]))
        do(dve.tensor_scalar(m.rinv[:], m.rinv[:], 0.5, None, ALU.mult))
        for k in range(TOPK):
            do(dve.tensor_reduce(m.best[k][:], m.ex[:], AX.X, ALU.max))
            do(dve.tensor_tensor(c.weight[:, k, :], m.best[k][:], m.rinv[:], ALU.mult))
            do(dve.tensor_tensor(m.eq[:], m.ex[:], tile_wide(m.best[k]), ALU.is_equal))
            do(dve.tensor_tensor(m.eq[:], m.eq[:], experts, ALU.mult))
            do(dve.tensor_reduce(m.row[:], m.eq[:], AX.X, ALU.min))
            do(dve.tensor_tensor(m.oh[k][:], experts, tile_wide(m.row), ALU.is_equal))
            if k + 1 < TOPK:
                do(dve.scalar_tensor_tensor(out=m.ex[:], in0=m.oh[k][:], scalar=-2.0, in1=m.ex[:],
                                            op0=ALU.mult, op1=ALU.add))
        dve.tensor_tensor(m.chosen[:].rearrange("p e t -> p t e"), m.oh[0][:], m.oh[1][:], ALU.add)\
           .then_inc(self.chosen_ready, 1)
        dve.wait_ge(self.ranked, 1)
        totals = bank[4][:, 0:E * NT]
        do(dve.tensor_tensor_scan(m.incl[:].rearrange("p e t -> p (e t)"), c.fresh[:].rearrange("p e t -> p (e t)"),
                                  totals, 0.0, ALU.mult, ALU.add))
        do(dve.tensor_tensor(m.place[:].rearrange("p e t -> p (e t)"), m.incl[:].rearrange("p e t -> p (e t)"),
                             totals, ALU.subtract))
        do(dve.tensor_tensor(m.place[:].rearrange("p e t -> p (e t)"), m.place[:].rearrange("p e t -> p (e t)"),
                             bank[5][:, 0:E * NT], ALU.add))
        do(dve.tensor_scalar(m.cnt[:], m.incl[:, :, NT - 1], float(P - 1), None, ALU.add))
        do(dve.tensor_scalar(m.tiles_i[:], m.cnt[:], 7, None, ALU.logical_shift_right))
        do(dve.tensor_copy(m.tiles[:], m.tiles_i[:]))
        do(dve.tensor_tensor_scan(m.endt[:], c.fresh[:, 0, 1:1 + E], m.tiles[:], 0.0, ALU.mult, ALU.add))
        do(dve.tensor_tensor(m.base[:], m.endt[:], m.tiles[:], ALU.subtract))
        do(dve.scalar_tensor_tensor(out=m.place[:], in0=m.base[:].unsqueeze(2).to_broadcast([P, E, NT]),
                                    scalar=float(P), in1=m.place[:], op0=ALU.mult, op1=ALU.add))
        for k in range(TOPK):
            do(dve.tensor_tensor(m.eq[:], m.oh[k][:], m.place[:].rearrange("p e t -> p t e"), ALU.mult))
            do(dve.tensor_reduce(m.posf[:, :, k], m.eq[:], AX.X, ALU.add))
        flat = m.posf[:].rearrange("p t k -> p (t k)")
        do(dve.tensor_copy(c.pos[:], flat))
        do(dve.tensor_scalar(m.slot_i[:], c.pos[:], 7, None, ALU.logical_shift_right))
        do(dve.tensor_copy(m.slot[:], m.slot_i[:]))
        do(dve.scalar_tensor_tensor(out=m.lane[:], in0=m.slot[:], scalar=-float(P), in1=flat,
                                    op0=ALU.mult, op1=ALU.add))
        ne = [P, NS, E]
        do(dve.tensor_tensor(m.past[:], c.slot_iota[:, 0:NS].unsqueeze(2).to_broadcast(ne),
                             m.endt[:].unsqueeze(1).to_broadcast(ne), ALU.is_ge))
        do(dve.tensor_reduce(m.wsel[:], m.past[:], AX.X, ALU.add))
        do(dve.tensor_scalar(m.woff[:], m.wsel[:], float(E - 1), float(WE), ALU.min, ALU.mult))

        with dve.Fori(0, NT // 8) as n:
            for c4 in range(4):
                for p in range(2):
                    i = 4 * n + c4
                    t = 2 * i + p
                    dve.wait_ge(self.hot_used[p], i)
                    for k in range(TOPK):
                        at = bass.ds(t * TOPK + k, 1)
                        dve.tensor_scalar(m.hot[p][:, k, :], c.slot_iota[:], m.lane[:, at], None, ALU.is_equal)\
                           .then_inc(self.hot_ready, 1)
                        dve.tensor_scalar(m.vals[p][:, k, :], c.slot_iota[:, 0:NS], m.slot[:, at],
                                          c.token[:, bass.ds(t, 1)], ALU.is_equal, ALU.mult)\
                           .then_inc(self.hot_ready, 1)
        dve.wait_ge(self.ids_done, 1)
        dve.tensor_copy(m.ids[:], bank[3][:, 0:NS]).then_inc(self.ids_ready, 1)

    def combine(self, dve):
        m, c = self.m, self.c
        with dve.Fori(0, NT // 8) as i:
            for p in range(2):
                dve.wait_ge(self.y_back[p], 16 * 4 * TOPK * i + 16 * 4 * TOPK)
                for k in range(TOPK):
                    if k:
                        dve.wait_ge(self.x_done, (4 * TOPK) * (2 * i + p) + 4)
                    for q in range(4):
                        t = 8 * i + (4 * p + q)
                        row = c.x[:, bass.ds(t, 1), :].rearrange("p a c -> p (a c)")
                        add = dve.scalar_tensor_tensor(out=row, in0=m.yg[p][:, q, k, :],
                                                       scalar=c.weight[:, k, bass.ds(t, 1)], in1=row,
                                                       op0=ALU.mult, op1=ALU.add)
                        add.then_inc(self.x_done, 1)
                dve.wait_ge(self.x_done, (4 * TOPK) * (2 * i + p) + 4 * TOPK)
                dve.sem_inc(self.yg_used[p], 4)

    def tensor(self, pe):
        m, c, bank, nc = self.m, self.c, self.c.bank, self.nc
        pe.wait_ge(c.const, c.CONSTS)
        pe.wait_ge(c.beta_ready, 1 + KC)
        for k in range(KC):
            nc.tensor.matmul(bank[6][:, 0:E], c.beta_rep[:, k, :], c.gw[:, k, :], start=k == 0, stop=k == KC - 1)

        def turn(i, p, q):
            pe.wait_ge(self.xf_ready, 8 * i + (4 * p + q + 1))
            for k in range(KC):
                last = nc.tensor.transpose(bank[q][:, k * P:(k + 1) * P], m.xf[p][:, q, k * P:(k + 1) * P], c.ident[:])
            last.then_inc(self.xf_in_psum, 1)

        def score(i, p, q):
            pe.wait_ge(self.xgt_ready, KC * (8 * i + (4 * p + q + 1)))
            for k in range(KC):
                last = nc.tensor.matmul(bank[7][:, bass.ds(8 * E * i + (4 * p + q) * E, E)], m.xgt[q][:, k, :],
                                        c.gw[:, k, :], start=k == 0, stop=k == KC - 1)
            last.then_inc(self.scored, 1)

        for q in range(4):
            turn(0, 0, q)
        with pe.Fori(0, NT // 8 - 1) as i:
            for p in range(2):
                for q in range(4):
                    score(i, p, q)
                    turn(i + p, 1 - p, q)
        last_round = NT // 8 - 1
        for q in range(4):
            score(last_round, 0, q)
            turn(last_round, 1, q)
        for q in range(4):
            score(last_round, 1, q)
        pe.wait_ge(self.scored, NT)
        pe.sem_inc(self.logits_done, 1)

        pe.wait_ge(self.chosen_ready, 1)
        flat = m.chosen[:].rearrange("p e t -> p (e t)")
        nc.tensor.matmul(bank[5][:, 0:E * NT], c.before[:], flat, start=True, stop=True)
        nc.tensor.matmul(bank[4][:, 0:E * NT], c.ones[:], flat, start=True, stop=True).then_inc(self.ranked, 1)

        acc = bank[3][:, 0:NS]
        nc.tensor.matmul(acc, c.zeros[:, 0:P], c.zeros[:, 0:NS], start=True, stop=False)
        with pe.Fori(0, NT // 8) as i:
            for n in range(8):
                pe.wait_ge(self.hot_ready, (2 * TOPK) * (8 * i + (n + 1)))
                for k in range(TOPK):
                    last = nc.tensor.matmul(acc, m.hot[n % 2][:, k, :], m.vals[n % 2][:, k, :],
                                            start=False, stop=False)
                last.then_inc(self.hot_used[n % 2], 1)
        nc.tensor.matmul(acc, c.zeros[:, 0:P], c.zeros[:, 0:NS], start=False, stop=True).then_inc(self.ids_done, 1)
        pe.wait_ge(self.lo_done, 2 * self.NCH)
        pe.wait_ge(self.ids_ready, 1)
        self.pe_tiles(pe)

    @staticmethod
    def rounds(eng, body):
        for j in range(-1, 4):
            body(j // 2, j % 2, (j >= 0, j >= 1, True, j >= 2))
        pairs = NS // 2 - 3
        unrolled = next(n for n in (3, 2, 1) if pairs % n == 0)
        with eng.Fori(0, pairs // unrolled) as n:
            for c in range(unrolled):
                for p in range(2):
                    body(unrolled * n + (2 + c), p, (True, True, True, True))
        for j in range(NS - 2, NS + 2):
            body(j // 2, j % 2, (j < NS, j <= NS, j + 1 < NS, True))

    def pe_tiles(self, pe):
        m, c, bank, nc = self.m, self.c, self.c.bank, self.nc
        xb, hb, tb, yb = bank[0:2], bank[2:4], bank[4:6], bank[6:8]

        def body(i, p, parts):
            j, o = 2 * i + p, 1 - p
            hidden, turn_h, turn_x, out = parts
            if hidden:
                off = pe.value_load(m.woff[0:1, bass.ds(j, 1)], min_val=0, max_val=(E - 1) * WE)
                pe.wait_ge(self.xt_lo, j + 1)
                pe.wait_ge(self.gelu_done, at_least(j - 1))
                for k in range(KC):
                    x = [m.xt[p][s][:, k * P:(k + 1) * P] for s in range(2)]
                    w = [m.w1[s][:, bass.ds(off + k * F, F)] for s in range(2)]
                    last = split_pass(nc, hb[p][:], x[0], x[1], w[0], w[1], k == 0, k == KC - 1)
                last.then_inc(self.h_done, 1)
            if turn_x:
                pe.wait_ge(self.gathered[o], 16 * (i + p) + 16)
                pe.wait_ge(self.xt_lo, at_least(j))
                for k in range(KC):
                    last = nc.tensor.transpose(xb[o][:, k * P:(k + 1) * P], m.xg[o][:, k * P:(k + 1) * P], c.ident[:])
                last.then_inc(self.xg_used[o], 1)
            if turn_h:
                pe.wait_ge(self.gelu_done, j)
                pe.wait_ge(self.ht_lo, at_least(j - 2))
                for k in range(KF):
                    last = nc.tensor.transpose(tb[o][:, k * P:(k + 1) * P], m.h[o][:, k * P:(k + 1) * P], c.ident[:])
                last.then_inc(self.h_turned, 1)
            if out:
                off = pe.value_load(m.woff[0:1, bass.ds(j - 2, 1)], min_val=0, max_val=(E - 1) * WE)
                pe.wait_ge(self.ht_lo, j - 1)
                pe.wait_ge(self.y_ready, at_least(j - 3))
                for k in range(KF):
                    h = [m.ht[p][s][:, k * P:(k + 1) * P] for s in range(2)]
                    w = [m.w2[s][:, bass.ds(off + k * C, C)] for s in range(2)]
                    last = split_pass(nc, yb[p][:, 0:C], h[0], h[1], w[0], w[1], k == 0, k == KF - 1)
                last.then_inc(self.y_done, 1)

        self.rounds(pe, body)

    def act_tiles(self, act):
        m, bank = self.m, self.c.bank
        xb, hb, tb = bank[0:2], bank[2:4], bank[4:6]

        def body(i, p, parts):
            j, o = 2 * i + p, 1 - p
            hidden, turn_h, turn_x, out = parts
            if hidden:
                act.wait_ge(self.h_done, j + 1)
                act.wait_ge(self.h_turned, at_least(j - 1))
                act.activation(m.h[p][:], hb[p][:], ACT.Gelu).then_inc(self.gelu_done, 1)
            if turn_x:
                act.wait_ge(self.xg_used[o], i + p + 1)
                act.wait_ge(self.h_done, at_least(j))
                act.activation(m.xt[o][0][:], xb[o][:, 0:C], ACT.Copy).then_inc(self.xt_hi, 1)
            if turn_h:
                act.wait_ge(self.h_turned, j)
                act.wait_ge(self.y_done, at_least(j - 2))
                act.activation(m.ht[o][0][:], tb[o][:], ACT.Copy).then_inc(self.ht_hi, 1)

        self.rounds(act, body)

    def dve_tiles(self, dve):
        m, bank = self.m, self.c.bank
        xb, tb, yb = bank[0:2], bank[4:6], bank[6:8]

        def body(i, p, parts):
            j, o = 2 * i + p, 1 - p
            hidden, turn_h, turn_x, out = parts
            if turn_x:
                dve.wait_ge(self.xt_hi, j + 2)
                dve.tensor_tensor(m.xt[o][1][:], xb[o][:, 0:C], m.xt[o][0][:].bitcast(F32), ALU.subtract)\
                   .then_inc(self.xt_lo, 1)
            if turn_h:
                dve.wait_ge(self.ht_hi, j)
                dve.tensor_tensor(m.ht[o][1][:], tb[o][:], m.ht[o][0][:].bitcast(F32), ALU.subtract)\
                   .then_inc(self.ht_lo, 1)
            if out:
                dve.wait_ge(self.y_done, j - 1)
                dve.wait_ge(self.y_stored[p], 16 * (i - 1))
                dve.tensor_copy(m.y[p][:], yb[p][:, 0:C]).then_inc(self.y_ready, 1)

        self.rounds(dve, body)




GH = 4
NG = HEADS // GH
SLOTS = HEADS // 2
QK_ROWS = 3 * DK
SCALE = (DK ** -0.5, 1.0)
SCORES = P * TB * (TB + 1) // 2
AT_QUERY = [10 * P, 8 * P, 4 * P, 0]
IN_ROWS = [9 * P, 7 * P, 4 * P, 0]
AT_KEY = [0, 4 * P, 8 * P, 7 * P]
LONGEST_FIRST = [3, 2, 1, 0]
BANK_READ = [1, 2, 4, 4]
HOLDS_SET = ("score", "turn", "skip")
USES_BANK = ("turn_x", "qk", "v", "out")
PAIRS = HEADS * DV // P
HALVES = 2


def steps_of_batch(first, last):
    others = {u: [] for u in range(PAIRS)}
    adds = {0: [("add", 0)], 1: [("add", 1)]} if not last else {}
    others[0] += [("v", 0, TB - 1, 0)]
    others[1] += [("v", 0, 0, 1), ("v", 0, 1, 1)]
    others[2] += [("v", 0, 2, 1)]
    others[3] += [("v", 0, 3, 1)]
    if not first:
        others[0][:0] = [("out", -1, i, 0) for i in (2, 3)]
        others[2][:0] = [("out", -1, i, 1) for i in (0, 1)]
        others[3][:0] = [("out", -1, 2, 1)]
        others[4] += [("out", -1, 3, 1)]
    others[6] += [("out", 0, 0, 0)]
    others[7] += [("out", 0, 1, 0)]
    if not last:
        adds[1] += [("moments", 1)]
        adds[2] = [("norm", 1)]
        others[3] += [("turn_x", 1, k) for k in range(KC)]
        others[4] += [("qk", 1, 0, t) for t in range(2)]
        others[5] += [("qk", 1, 1, t) for t in range(2)]
        others[6] += [("v", 1, i, 0) for i in (0, 1)]
        others[7] += [("v", 1, 2, 0)]
    order = []

    def turn(d, h, u):
        return [("turn", d, h), ("copy", d, h, u)]

    for u in range(PAIRS):
        h = 2 * u
        pair = [(0, u - 2)] if u >= 2 else [] if first else [(-1, u - 2 + PAIRS)]
        before = turn(0, h - 1, u) if u else [("skip",)] if first else turn(-1, HEADS - 1, u)
        early, late = others[u][:1], others[u][1:]
        order += [("score", 0, h), ("score", 0, h + 1), *[("values", *p) for p in pair],
                  ("max", 0, h), ("max", 0, h + 1), ("exp", 0, h), ("normal", 0, h), ("exp", 0, h + 1),
                  *early, *before, *[("high", *p) for p in pair], *[("low", *p) for p in pair],
                  *late, ("normal", 0, h + 1), *turn(0, h, u), *adds.get(u, [])]
    if last:
        order += [*turn(0, HEADS - 1, PAIRS), ("skip",)]
        for pair in (PAIRS - 2, PAIRS - 1):
            order += [("values", 0, pair), ("high", 0, pair), ("low", 0, pair)]
        order += [("out", 0, i, 0) for i in (2, 3)] + [("out", 0, i, 1) for i in range(TB)]
    return order


def before_batches():
    return [("add", 0), ("add", 1), ("moments", 1), ("norm", 1), *[("turn_x", 1, k) for k in range(KC)],
            *[("qk", 1, w, t) for w in range(2) for t in range(2)], *[("v", 1, i, 0) for i in range(TB - 1)]]


def by_vector(h):
    return h % 2 == 1


def numbered(order):
    n, other, at = 0, 0, {}
    for kind, *a in order:
        if kind in HOLDS_SET:
            at[(kind, *a)] = n
            yield n, (kind, *a)
            n += 1
        elif kind in USES_BANK:
            yield other, (kind, *a)
            other += 1
        elif kind in ("max", "exp", "normal"):
            yield at[("score", *a)], (kind, *a)
        elif kind == "copy":
            yield at[("turn", *a[:2])], (kind, *a)
        else:
            yield n, (kind, *a)


W_SIZES = {"wq": KC * HEADS * DK, "wk": KC * HEADS * DK, "wv": KC * HEADS * DV, "wo": PAIRS * C}
W_COLS = sum(W_SIZES.values())
W_CHUNKS = 8
W_CHUNK = W_COLS // W_CHUNKS


class AttentionMemory:
    def __init__(self, nc, ctx):
        def sb(name, shape, dt):
            return ctx.enter_context(nc.sbuf_tensor(name, shape, dt))

        def parts(name, shape):
            return [sb(f"{name}_{x}", shape, F32R) for x in ("hi", "lo")]

        self.v = sb("v_rows", [P, TB, HEADS * DV], F32)
        self.weights = parts("attention_w", [P, W_COLS])
        self.rows = [sb(f"p_rows{i}", [P, SCORES], F32) for i in range(3)]
        at = 0
        views = {}
        for name, size in W_SIZES.items():
            wide = C if name == "wo" else size // KC
            views[name] = [w[:, at:at + size].rearrange("p (k n) -> p k n", n=wide) for w in self.weights]
            at += size
        self.wq, self.wk, self.wv, self.wo = views["wq"], views["wk"], views["wv"], views["wo"]
        self.q = sb("q_rows", [P, SLOTS, T], F32R)
        self.k = sb("k_rows", [P, SLOTS, T], F32R)
        self.stats = sb("a_stats", [P, TB, 6], F32)
        self.mv = sb("a_mv", [P, 2, TB], F32)
        self.var = sb("a_var", [P, TB], F32)
        self.rstd = sb("a_rstd", [P, TB], F32)
        self.xt = parts("xnt", [P, KC, T])
        shared = sb("xn_or_qk0", [P, 2, T], F32R)
        self.xn = shared[:].bitcast(F32).rearrange("p a (b c) -> p (a b) c", c=C)
        self.staged = [[shared[:, 0, :], shared[:, 1, :]], parts("qk1", [P, T])]
        self.turned = [sb(f"p_turned{i}", [P, SCORES], F32) for i in range(3)]
        self.negmax = sb("negmax", [P, TB, GH], F32)
        self.sums = sb("sums", [P, TB, GH], F32)
        self.factor = sb("factor", [P, TB], F32)
        self.ct = parts("ctx", [P, PAIRS, T])
        self.ident_b = sb("ident_b", [P, P], BF16)
        self.hide_keys = sb("hide_keys", [P, P], BF16)

    def rows_of(self, h):
        return self.rows[0 if h % 2 == 0 else 1 + h // 2 % 2]

    def turned_of(self, h):
        return self.turned[0 if h % 2 else 1 + h // 2 % 2]


class Attention:

    CONSTS = 4

    def __init__(self, core, mem, mixture):
        self.c, self.m, self.nc = core, mem, core.nc
        self.y_d = mixture.y_d

        def sem(name):
            return core.sem(f"at_{name}")

        def two(name):
            return [sem(f"{name}{i}") for i in range(2)]

        self.rows_d = [self.nc.dram_tensor(f"{w}_rows_d", [QK_ROWS, HEADS, T], F32, kind="Internal") for w in "qk"]
        self.w_in = [sem(f"w_in{i}") for i in range(STAGED)]
        self.w_hi = sem("w_hi")
        self.w_lo = sem("w_lo")
        self.const = sem("const")
        self.y_ids_ready = sem("y_ids_ready")
        self.y_in = sem("y_in")
        self.x_added = sem("x_added")
        self.stats_done = sem("stats_done")
        self.mv_done = sem("mv_done")
        self.var_ready = sem("var_ready")
        self.rstd_ready = sem("rstd_ready")
        self.xn_ready = sem("xn_ready")
        self.set_full = sem("set_full")
        self.set_free = two("set_free")
        self.bank_full = sem("bank_full")
        self.bank_free = sem("bank_free")
        self.high_ready = sem("high_ready")
        self.staged_out = two("staged_out")
        self.rows_in = [sem(f"rows_in{g}") for g in range(NG)]
        self.rows_read = sem("rows_read")
        self.maxima = sem("maxima")
        self.factor_ready = sem("factor_ready")
        self.normal = sem("normal")
        self.pv_done = sem("pv_done")
        self.ctx_high = sem("ctx_high")
        self.ctx_split = sem("ctx_split")
        self.orders = [before_batches(), *[steps_of_batch(*x) for x in ((True, False), (False, False), (False, True))]]
        self.held = [sum(s[0] in HOLDS_SET for s in o) for o in self.orders]
        self.used = [sum(s[0] in USES_BANK for s in o) for o in self.orders]
        assert all(h % 2 == 0 for h in self.held)

    def before(self, counts, b):
        start, first, body, _ = counts
        return 0 if isinstance(b, int) and b < 0 else start if isinstance(b, int) and b == 0 else \
            body * b + (start + first - body)

    def batches(self, eng, walk):
        start, first, body, last = self.orders
        walk(-1, start)
        walk(0, first)
        with eng.Fori(1, B - 1) as b:
            walk(b, body)
        walk(B - 1, last)

    def wait_all(self, eng):
        for s in range(2):
            eng.wait_ge(self.set_free[s], (self.before(self.held, B - 1) + self.held[-1]) // 2)
        eng.wait_ge(self.bank_free, self.before(self.used, B - 1) + self.used[-1])

    def half_held(self, b):
        return self.before([h // 2 for h in self.held], b)

    def wait_set(self, eng, b, n):
        eng.wait_ge(self.set_free[n % 2], self.half_held(b) + (n // 2 + 1))

    def wait_full(self, eng, b, n):
        eng.wait_ge(self.set_full, self.before(self.held, b) + (n + 1))

    def wait_bank(self, eng, b, n):
        eng.wait_ge(self.bank_full, self.before(self.used, b) + (n + 1))

    def wait_bank_free(self, eng, b, n):
        number = self.before(self.used, b) + n
        if not isinstance(number, int) or number:
            eng.wait_ge(self.bank_free, number)

    def pool(self, pool):
        m = self.m
        s = Steps(pool, self.const)
        s.did(pool.memset(m.ident_b[:], 0.0))
        s.did(pool.memset(m.hide_keys[:], 0.0))
        s.settle()
        s.did(pool.affine_select(out=m.ident_b[:], in_=m.ident_b[:], compare_op=ALU.not_equal, fill=1.0,
                                 base=0, pattern=[[-1, P]], channel_multiplier=1))
        s.did(pool.affine_select(out=m.hide_keys[:], in_=m.hide_keys[:], compare_op=ALU.is_ge, fill=NEG,
                                 base=0, pattern=[[-1, P]], channel_multiplier=1))
        assert s.k == self.CONSTS

        def walk(b, order):
            for _, (kind, *a) in numbered(order):
                if kind == "add":
                    self.gather(pool, b, a[0])
                elif kind == "moments":
                    pool.wait_ge(self.var_ready, b + 2)
                    pool.tensor_tensor(m.rstd[:], m.var[:], self.c.minus_half[:, 0:TB], ALU.pow)\
                        .then_inc(self.rstd_ready, 1)

        self.batches(pool, walk)

    def gather(self, pool, b, half):
        c = self.c
        number = 2 * b + (2 + half)
        if not isinstance(number, int) or number:
            pool.wait_ge(self.x_added, 2 * TOPK * number)
        at = TOPK * TB * b + (TOPK * TB + 2 * TOPK * half)
        pool.tensor_copy(c.y_ids[:], c.pos[:, bass.ds(at, 2 * TOPK)]).then_inc(self.y_ids_ready, 1)
        pool.wait_ge(self.y_ids_ready, number + 1)
        pool.sem_inc(self.c.waited, 1)
        for q in range(2 * TOPK):
            pool.indirect_dma_start(out=c.y_pair[:, q // TOPK, q % TOPK, :], out_offset=None, in_=self.y_d[:],
                                    in_offset=bass.IndirectOffsetOnAxis(ap=c.y_ids[:, q:q + 1], axis=0))\
                .then_inc(self.y_in, 16)

    def add(self, dve, b, half):
        c = self.c
        number = 2 * b + (2 + half)
        dve.wait_ge(self.y_in, 32 * TOPK * number + 32 * TOPK)
        for k in range(TOPK):
            if k:
                dve.wait_ge(self.x_added, 2 * TOPK * number + 2)
            for q in range(2):
                t = TB * b + (TB + 2 * half + q)
                row = c.x[:, bass.ds(t, 1), :].rearrange("p a c -> p (a c)")
                dve.scalar_tensor_tensor(out=row, in0=c.y_pair[:, q, k, :], scalar=c.weight[:, k, bass.ds(t, 1)],
                                         in1=row, op0=ALU.mult, op1=ALU.add).then_inc(self.x_added, 1)

    def sync_weights(self, sp):
        for n in range(W_CHUNKS):
            if n >= STAGED:
                sp.wait_ge(self.w_lo, n - STAGED + 1)
            sp.dma_start(self.m.rows[n % STAGED][:, 0:W_CHUNK], self.c.ins["attention_w"][:, n * W_CHUNK:(n + 1) * W_CHUNK])\
              .then_inc(self.w_in[n % STAGED], 16)

    def act_weights(self, act):
        for n in range(W_CHUNKS):
            act.wait_ge(self.w_in[n % STAGED], 16 * (n // STAGED + 1))
            act.activation(self.m.weights[0][:, n * W_CHUNK:(n + 1) * W_CHUNK], self.m.rows[n % STAGED][:, 0:W_CHUNK],
                           ACT.Copy).then_inc(self.w_hi, 1)

    def dve_weights(self, dve, chunks):
        for n in chunks:
            cut = slice(n * W_CHUNK, (n + 1) * W_CHUNK)
            dve.wait_ge(self.w_hi, n + 1)
            dve.tensor_tensor(self.m.weights[1][:, cut], self.m.rows[n % STAGED][:, 0:W_CHUNK],
                              self.m.weights[0][:, cut].bitcast(F32), ALU.subtract).then_inc(self.w_lo, 1)

    def sync(self, sp):
        m = self.m
        def store_rows(w, t):
            which = (0, 1, 0) if w == 0 else (0, 0, 1)
            for r in range(3):
                there = self.rows_d[w][r * DK:(r + 1) * DK, t * SLOTS:(t + 1) * SLOTS, :]
                sp.dma_start(there.rearrange("p h n -> h p n"), m.staged[t][which[r]][:, 0:T].bitcast(F32))\
                  .then_inc(self.staged_out[t], 16)

        def load_rows(b):
            for t in range(2):
                sp.wait_ge(self.staged_out[t], 96 * (b + 2))
            for g in range(NG):
                if not isinstance(b, int) or b >= 0:
                    sp.wait_ge(self.rows_read, HEADS * b + GH * (g + 1))
                for par in range(2):
                    for w, rows in ((0, m.q), (1, m.k)):
                        src = self.rows_d[w][:].rearrange("r (s two) n -> r s two n", two=2)
                        sp.dma_start(rows[64 * par:64 * par + QK_ROWS, 2 * g:2 * g + 2, :].bitcast(F32),
                                     src[:, 2 * g:2 * g + 2, par, :]).then_inc(self.rows_in[g], 16)

        def walk(b, order):
            for n, (kind, *a) in numbered(order):
                if kind == "qk":
                    _, w, t = a
                    if w == 0 and t == 0 and (not isinstance(b, int) or b >= 0):
                        for g in range(NG):
                            sp.wait_ge(self.rows_in[g], 64 * (b + 1))
                        sp.sem_inc(self.c.waited, 1)
                    sp.wait_ge(self.bank_free, self.before(self.used, b) + (n + 1))
                    store_rows(w, t)
                    if w == 1 and t == 1:
                        load_rows(b)

        self.batches(sp, walk)

    def scalar(self, act):
        m, sets, bank = self.m, self.c.sets, self.c.bank[7]
        act.wait_ge(self.w_lo, W_CHUNKS)

        def walk(b, order):
            for n, (kind, *a) in numbered(order):
                s = sets[n % 2]
                if kind in ("turn_x", "qk", "v"):
                    self.wait_bank(act, b, n)
                if kind == "turn_x":
                    act.activation(m.xt[0][:, a[1], :], bank, ACT.Copy).then_inc(self.high_ready, 1)
                elif kind == "qk":
                    _, w, t = a
                    if w or not isinstance(b, int) or b >= 0:
                        act.wait_ge(self.staged_out[t], 96 * (b + 1) + 48 * w)
                    act.activation(m.staged[t][0][:, 0:T], bank, ACT.Copy, scale=SCALE[w]).then_inc(self.high_ready, 1)
                elif kind == "v":
                    _, i, half = a
                    act.activation(m.v[:, i, half * T:(half + 1) * T], bank, ACT.Copy).then_inc(self.bank_free, 1)
                elif kind == "exp":
                    _, h = a
                    for k, i in enumerate(LONGEST_FIRST):
                        if k < TB - 1:
                            act.wait_ge(self.maxima, TB * (HEADS * b + h) + BANK_READ[k])
                        last = act.activation(m.rows_of(h)[:, IN_ROWS[i]:IN_ROWS[i] + (i + 1) * P],
                                              s[:, AT_QUERY[i]:AT_QUERY[i] + (i + 1) * P], ACT.Exp,
                                              bias=m.negmax[:, i, h % GH:h % GH + 1],
                                              accum_out=m.sums[:, i, h % GH:h % GH + 1])
                    last.then_inc(self.set_free[n % 2], 1)
                elif kind == "copy":
                    d, h, u = a
                    if not by_vector(h):
                        self.wait_full(act, b, n)
                        self.wait_turned(act, b, u)
                        act.activation(m.turned_of(h)[:], s[:, 0:SCORES], ACT.Copy).then_inc(self.set_free[n % 2], 1)
                elif kind == "high":
                    d, pair = a
                    act.wait_ge(self.pv_done, PAIRS * b + (PAIRS * d + pair + 1))
                    act.activation(m.ct[0][:, pair, :], self.c.bank[6], ACT.Copy).then_inc(self.ctx_high, 1)

        self.batches(act, walk)

    def wait_turned(self, eng, b, u):
        if not isinstance(b, int) or PAIRS * b + u > 1:
            eng.wait_ge(self.pv_done, PAIRS * b + (u - 1))

    HIGHS = KC + 4

    def vector(self, dve):
        m, sets, c, bank = self.m, self.c.sets, self.c, self.c.bank[7]

        def highs(b, k):
            dve.wait_ge(self.high_ready, self.HIGHS * b + (self.HIGHS + k + 1))

        def row(b, t):
            return c.x[:, TB * b + t, :] if isinstance(b, int) else \
                c.x[:, bass.ds(TB * b + t, 1), :].rearrange("p a c -> p (a c)")

        def walk(b, order):
            k = 0
            for n, (kind, *a) in numbered(order):
                s, free = sets[n % 2], self.set_free[n % 2]
                if kind in ("max", "skip"):
                    self.wait_full(dve, b, n)
                if kind == "add":
                    if isinstance(b, int) and b < 0:
                        half_chunks = W_CHUNKS // 2
                        self.dve_weights(dve, range(a[0] * half_chunks, (a[0] + 1) * half_chunks))
                    self.add(dve, b, a[0])
                elif kind == "moments":
                    dve.wait_ge(self.x_added, 4 * TOPK * (b + 2))
                    dve.sem_inc(self.c.waited, 1)
                    for i in range(TB):
                        dve.bn_stats(m.stats[:, i, :], row(b, TB + i)).then_inc(self.stats_done, 1)
                    dve.wait_ge(self.stats_done, TB * (b + 2))
                    dve.sem_inc(self.c.waited, 1)
                    for i in range(TB):
                        dve.bn_aggr(m.mv[:, :, i], m.stats[:, i, :]).then_inc(self.mv_done, 1)
                    dve.wait_ge(self.mv_done, TB * (b + 2))
                    dve.tensor_scalar(m.var[:], m.mv[:, 1, :], EPS, None, ALU.add).then_inc(self.var_ready, 1)
                elif kind == "norm":
                    dve.wait_ge(self.rstd_ready, b + 2)
                    if not isinstance(b, int) or b >= 0:
                        dve.wait_ge(self.staged_out[0], 96 * (b + 1))
                    for i in range(TB):
                        dve.tensor_scalar(m.xn[:, i, :], row(b, TB + i), m.mv[:, 0, i:i + 1], m.rstd[:, i:i + 1],
                                          ALU.subtract, ALU.mult).then_inc(self.xn_ready, 1)
                elif kind == "turn_x":
                    highs(b, k)
                    k += 1
                    dve.tensor_tensor(m.xt[1][:, a[1], :], bank, m.xt[0][:, a[1], :].bitcast(F32),
                                      ALU.subtract).then_inc(self.bank_free, 1)
                elif kind == "qk":
                    _, w, t = a
                    highs(b, k)
                    k += 1
                    dve.scalar_tensor_tensor(out=m.staged[t][1][:, 0:T], in0=bank, scalar=SCALE[w],
                                             in1=m.staged[t][0][:, 0:T].bitcast(F32), op0=ALU.mult, op1=ALU.subtract)\
                       .then_inc(self.bank_free, 1)
                elif kind == "max":
                    _, h = a
                    for i in LONGEST_FIRST:
                        dve.tensor_reduce(m.negmax[:, i, h % GH:h % GH + 1],
                                          s[:, AT_QUERY[i]:AT_QUERY[i] + (i + 1) * P],
                                          AX.X, ALU.max, negate=True).then_inc(self.maxima, 1)
                elif kind == "normal":
                    _, h = a
                    number = HEADS * b + h
                    self.wait_set(dve, b, n)
                    if not isinstance(number, int) or number:
                        dve.wait_ge(self.normal, number)
                    dve.reciprocal(m.factor[:], m.sums[:, :, h % GH]).then_inc(self.factor_ready, 1)
                    dve.wait_ge(self.factor_ready, number + 1)
                    for i in range(TB):
                        cut = slice(IN_ROWS[i], IN_ROWS[i] + (i + 1) * P)
                        last = dve.tensor_scalar(m.rows_of(h)[:, cut], m.rows_of(h)[:, cut], m.factor[:, i:i + 1],
                                                 None, ALU.mult)
                    last.then_inc(self.normal, 1)
                elif kind == "copy":
                    d, h, u = a
                    if by_vector(h):
                        self.wait_full(dve, b, n)
                        self.wait_turned(dve, b, u)
                        dve.tensor_copy(m.turned_of(h)[:], s[:, 0:SCORES]).then_inc(free, 1)
                elif kind == "low":
                    d, pair = a
                    dve.wait_ge(self.ctx_high, PAIRS * b + (PAIRS * d + pair + 1))
                    dve.tensor_tensor(m.ct[1][:, pair, :], c.bank[6], m.ct[0][:, pair, :].bitcast(F32),
                                      ALU.subtract).then_inc(self.ctx_split, 1)
                elif kind == "out":
                    d, i, _ = a
                    self.wait_bank(dve, b, n)
                    dve.tensor_tensor(row(b, TB * d + i), row(b, TB * d + i), bank[:, 0:C], ALU.add)\
                       .then_inc(self.bank_free, 1)
                elif kind == "skip":
                    dve.sem_inc(free, 1)

        self.batches(dve, walk)
        self.wait_all(dve)

    def tensor(self, pe):
        m, sets, c, nc, bank = self.m, self.c.sets, self.c, self.nc, self.c.bank[7]
        pe.wait_ge(self.w_lo, W_CHUNKS)
        pe.wait_ge(self.const, self.CONSTS)

        def score(s, q, k):
            for i in LONGEST_FIRST:
                read = nc.tensor.matmul(s[:, AT_QUERY[i]:AT_QUERY[i] + (i + 1) * P], q[:, i * P:(i + 1) * P],
                                        k[:, 0:(i + 1) * P], start=i != 0, stop=False, skip_group_check=True)
            for i in LONGEST_FIRST:
                at = AT_QUERY[i] + i * P
                last = nc.tensor.matmul(s[:, at:at + P], m.ident_b[:], m.hide_keys[:], start=False, stop=True,
                                        skip_group_check=True)
            return read, last

        def head(x, h):
            at = 64 * (h % 2)
            return x[at:at + QK_ROWS, h // 2, :]

        def walk(b, order):
            for n, (kind, *a) in numbered(order):
                s = sets[n % 2]
                if kind in HOLDS_SET and (b != 0 if isinstance(b, int) else True) or kind in HOLDS_SET and n >= 2:
                    pe.wait_ge(self.set_free[n % 2], self.half_held(b) + n // 2)
                if kind in USES_BANK:
                    self.wait_bank_free(pe, b, n)
                if kind == "turn_x":
                    pe.wait_ge(self.xn_ready, TB * (b + 2))
                    k = a[1]
                    for i in range(TB):
                        last = nc.tensor.transpose(bank[:, i * P:(i + 1) * P], m.xn[:, i, k * P:(k + 1) * P],
                                                   c.ident[:])
                elif kind == "qk":
                    _, w, t = a
                    w = (m.wq, m.wk)[w]
                    for k in range(KC):
                        last = split_pass(nc, bank, w[0][:, k, t * P:(t + 1) * P], w[1][:, k, t * P:(t + 1) * P],
                                          m.xt[0][:, k, :], m.xt[1][:, k, :], k == 0, k == KC - 1)
                elif kind == "v":
                    _, i, half = a
                    cut = slice(half * T, (half + 1) * T)
                    for k in range(KC):
                        last = split_pass(nc, bank, m.xt[0][:, k, i * P:(i + 1) * P],
                                          m.xt[1][:, k, i * P:(i + 1) * P], m.wv[0][:, k, cut], m.wv[1][:, k, cut],
                                          k == 0, k == KC - 1)
                elif kind == "score":
                    _, h = a
                    if h % GH == 0:
                        pe.wait_ge(self.rows_in[h // GH], 64 * (b + 1))
                    read, last = score(s, head(m.q, h), head(m.k, h))
                    read.then_inc(self.rows_read, 1)
                elif kind == "turn":
                    d, h = a
                    pe.wait_ge(self.normal, HEADS * b + (HEADS * d + h + 1))
                    for j in range(TB):
                        for i in range(j, TB):
                            key, query = AT_KEY[j] + (i - j) * P, IN_ROWS[i] + j * P
                            last = nc.tensor.transpose(s[:, key:key + P], m.rows_of(h)[:, query:query + P], c.ident[:])
                elif kind == "values":
                    d, pair = a
                    number = PAIRS * b + (PAIRS * d + pair)
                    if not isinstance(number, int) or number > 0:
                        pe.wait_ge(self.ctx_split, number)
                    if isinstance(b, int) and b == B - 1 and (d, pair) == (0, PAIRS - 1):
                        self.wait_set(pe, b, n - 2)
                    for j in range(TB):
                        for k in range(2):
                            at = (2 * pair + k) * DV
                            pv = nc.tensor.matmul(c.bank[6][k * DV:(k + 1) * DV, j * P:T],
                                                  m.v[:, j, at:at + DV],
                                                  m.turned_of(2 * pair + k)[:, AT_KEY[j]:AT_KEY[j] + (TB - j) * P],
                                                  start=j == 0, stop=j == TB - 1)
                    pv.then_inc(self.pv_done, 1)
                elif kind == "out":
                    d, i, half = a
                    half_pairs = PAIRS // HALVES
                    pe.wait_ge(self.ctx_split, PAIRS * b + (PAIRS * d + half_pairs * (half + 1)))
                    cut = slice(i * P, (i + 1) * P)
                    for k in range(half * half_pairs, (half + 1) * half_pairs):
                        last = split_pass(nc, bank[:, 0:C], m.ct[0][:, k, cut], m.ct[1][:, k, cut], m.wo[0][:, k, :],
                                          m.wo[1][:, k, :], k % half_pairs == 0, (k + 1) % half_pairs == 0)
                elif kind == "skip":
                    last = nc.tensor.transpose(s[:, 0:P], c.ident[:], c.ident[:])
                if kind in HOLDS_SET:
                    last.then_inc(self.set_full, 1)
                elif kind in USES_BANK:
                    last.then_inc(self.bank_full, 1)

        self.batches(pe, walk)


def layout(inputs, np):
    a = {k: np.ascontiguousarray(np.asarray(v)) for k, v in inputs.items()}

    def rows(w, k):
        return np.ascontiguousarray(w.reshape(k, P, -1).transpose(1, 0, 2))

    w1 = a["L0_ffn_w1"].transpose(0, 2, 1).reshape(E, KC, P, F).transpose(2, 0, 1, 3)
    w2 = a["L0_ffn_w2"].transpose(0, 2, 1).reshape(E, KF, P, C).transpose(2, 0, 1, 3)
    return {
        "x": a["L0_attn_x"].reshape(N, C),
        "gate": rows(a["L0_ffn_gate_w"].T, KC),
        "gamma": np.ascontiguousarray(a["L0_ffn_ln_gamma"].reshape(KC, P).T),
        "beta": np.ascontiguousarray(a["L0_ffn_ln_beta"].reshape(KC, P).T),
        "w1": np.ascontiguousarray(w1).reshape(P, E * WE),
        "w2": np.ascontiguousarray(w2).reshape(P, E * WE),
        "attention_w": np.concatenate([rows(a["L0_attn_" + w], k).reshape(P, -1)
                                       for w, k in (("Wq", KC), ("Wk", KC), ("Wv", KC), ("Wo", PAIRS))], axis=1),
    }


def build(nc, ins, out):
    with ExitStack() as ctx:
        core = Core(nc, ctx, ins)
        with ExitStack() as scope:
            moe_memory = MoeMemory(nc, scope)
        with ExitStack() as scope:
            attention_memory = AttentionMemory(nc, scope)
        first = Moe(core, moe_memory, "moe1")
        attention = Attention(core, attention_memory, first)
        second = Moe(core, moe_memory, "moe2")
        stored = core.sem("out_stored")
        block = ctx.enter_context(nc.Block())

        after_first = first.wait_stored

        @block.sync
        def _(sp):
            core.sync(sp)
            first.sync(sp)
            after_first(sp)
            attention.sync_weights(sp)
            attention.sync(sp)
            attention.wait_all(sp)
            second.sync(sp)
            rows, there = core.x, out.rearrange("(t p) c -> p t c", p=P)
            with sp.Fori(0, NT // 4) as g:
                sp.wait_ge(core.small, 48)
                sp.wait_ge(second.x_done, 4 * TOPK * g + 4 * TOPK)
                sp.dma_start(there[:, bass.ds(g * 4, 4), :], rows[:, bass.ds(g * 4, 4), :]).then_inc(stored, 16)
            sp.wait_ge(stored, 16 * (NT // 4))

        @block.gpsimd
        def _(pool):
            core.pool(pool)
            first.pool(pool)
            after_first(pool)
            attention.pool(pool)
            attention.wait_all(pool)
            second.pool(pool)
            second.gather_results(pool)

        @block.scalar
        def _(act):
            first.scalar(act)
            after_first(act)
            attention.act_weights(act)
            attention.scalar(act)
            attention.wait_all(act)
            second.scalar(act)

        @block.vector
        def _(dve):
            core.vector(dve)
            first.vector(dve)
            after_first(dve)
            attention.vector(dve)
            second.vector(dve)
            second.combine(dve)

        @block.tensor
        def _(pe):
            first.tensor(pe)
            after_first(pe)
            attention.tensor(pe)
            attention.wait_all(pe)
            second.tensor(pe)


def kernel(**inputs):
    import numpy as np
    import concourse.bacc as bacc
    from concourse.bass_utils import run_bass_kernel_spmd

    arrays = {f"in_{name}": a for name, a in layout(inputs, np).items()}
    nc = bacc.Bacc("TRN2", target_bir_lowering=False, num_devices=1)
    ins = {name[3:]: nc.dram_tensor(name, a.shape, mybir.dt.from_np(a.dtype), kind="ExternalInput").ap()
           for name, a in arrays.items()}
    out = nc.dram_tensor("out_rows", [N, C], F32, kind="ExternalOutput").ap()
    build(nc, ins, out)
    r = run_bass_kernel_spmd(nc, [arrays], core_ids=[0])
    return r.results[0]["out_rows"].reshape(B, T, C)
```
